# Optimizing a Trainium2 kernel written in Bass

```python
import numpy as np
import jax
import jax.numpy as jnp

def _softmax(x, axis=-1):
    return jax.nn.softmax(x, axis=axis)

def _gelu(x):
    return jax.nn.gelu(x, approximate=True)

def _silu(x):
    return jax.nn.silu(x)

def _sigmoid(x):
    return jax.nn.sigmoid(x)

def _layernorm(x, axis=-1, eps=1e-05):
    m = jnp.mean(x, axis=axis, keepdims=True)
    v = jnp.var(x, axis=axis, keepdims=True)
    return (x - m) / jnp.sqrt(v + eps)

def _scatter_add(tgt, idx, src, axis=0):
    return tgt.at[idx].add(src)

def _segment_sum(src, seg, n):
    return jax.ops.segment_sum(src, seg, n)
kernel_name = 'mk_gnn_resnorm_d2_gnn_r8_93a449'

def setup_inputs(seed: int=0):
    np.random.seed(seed)
    _w = jnp.asarray

    def _rec_inputs():
        import jax
        import jax.numpy as jnp
        _gk = jax.random.key(seed)
        x = -0.000202 + 1 * jax.random.normal(jax.random.fold_in(_gk, 1), (12500, 64), jnp.float32)
        src = jax.random.randint(jax.random.fold_in(_gk, 2), (400000,), 0, 12500, jnp.int32)
        dst = jnp.minimum((12500 * jax.random.uniform(jax.random.fold_in(_gk, 3), (400000,)) ** 2.0).astype(jnp.int32), 99999)
        _o = jnp.argsort(dst, stable=True)
        src = src[_o]
        dst = dst[_o]
        edge_attr_16 = 0.000312547 + 1.00004 * jax.random.normal(jax.random.fold_in(_gk, 12), (400000, 16), jnp.float32)
        return (x, src, dst, edge_attr_16)
    x, src, dst, edge_attr_16 = _rec_inputs()

    def _L0_gnn_setup():
        import jax, jax.numpy as jnp
        import numpy as np
        N_NODES = 12500
        N_EDGES = 150000
        D_IN = 64
        D_HID = 64

        def _norms(src, dst):
            ones = jnp.ones((src.shape[0],), jnp.float32)
            out_deg = jax.ops.segment_sum(ones, src, num_segments=N_NODES)
            in_deg = jax.ops.segment_sum(ones, dst, num_segments=N_NODES)
            out_norm = jax.lax.rsqrt(jnp.maximum(out_deg, 1.0))
            in_norm = jax.lax.rsqrt(jnp.maximum(in_deg, 1.0))
            return (out_norm, in_norm)

        def _graph_conv(x, src, dst, out_norm, in_norm, W, b):
            h = x * out_norm[:, None]
            agg = jax.ops.segment_sum(h[src], dst, num_segments=N_NODES)
            agg = agg * in_norm[:, None]
            return agg @ W + b
        key = jax.random.key(seed)
        ks = jax.random.split(key, 9)
        feat = jax.random.normal(ks[0], (N_NODES, D_IN), dtype=jnp.float32)
        src = jax.random.randint(ks[1], (N_EDGES,), 0, N_NODES)
        dst = jax.random.randint(ks[2], (N_EDGES,), 0, N_NODES)
        s = 1.0 / np.sqrt(D_IN)
        W0 = jax.random.normal(ks[3], (D_IN, D_HID), dtype=jnp.float32) * s
        W1 = jax.random.normal(ks[4], (D_HID, D_HID), dtype=jnp.float32) * s
        W2 = jax.random.normal(ks[5], (D_HID, D_HID), dtype=jnp.float32) * s
        b0 = jnp.zeros((D_HID,), jnp.float32)
        b1 = jnp.zeros((D_HID,), jnp.float32)
        b2 = jnp.zeros((D_HID,), jnp.float32)
        return {'feat': feat, 'W0': W0, 'b0': b0, 'W1': W1, 'b1': b1, 'W2': W2, 'b2': b2, 'src': src, 'dst': dst}
    _L0_gnn_all = _L0_gnn_setup()
    _L0_gnn_in = {k: v for k, v in _L0_gnn_all.items() if k in ('W0', 'b0', 'W1', 'b1', 'W2', 'b2')}
    del _L0_gnn_all

    def _L1_gnn_setup():
        import jax, jax.numpy as jnp
        import numpy as np
        N_NODES = 6250
        N_EDGES = 125000
        IN_SIZE = 64
        OUT_SIZE = 64
        EDGE_DIM = 16
        BN_EPS = 1e-05
        GIN_EPS = 0.0
        key = jax.random.key(seed)
        ks = jax.random.split(key, 10)
        s = 1.0 / np.sqrt(IN_SIZE)
        return {'x': jax.random.normal(ks[0], (N_NODES, IN_SIZE), dtype=jnp.float32), 'edge_index': jax.random.randint(ks[1], (2, N_EDGES), 0, N_NODES, dtype=jnp.int64), 'edge_attr': jax.random.normal(ks[2], (N_EDGES, EDGE_DIM), dtype=jnp.float32), 'W_edge': jax.random.uniform(ks[3], (IN_SIZE, EDGE_DIM), jnp.float32, -s, s), 'b_edge': jnp.zeros((IN_SIZE,), jnp.float32), 'W1': jax.random.uniform(ks[4], (OUT_SIZE, IN_SIZE), jnp.float32, -s, s), 'b1': jnp.zeros((OUT_SIZE,), jnp.float32), 'gamma': jnp.ones((OUT_SIZE,), jnp.float32), 'beta': jnp.zeros((OUT_SIZE,), jnp.float32), 'W2': jax.random.uniform(ks[5], (OUT_SIZE, OUT_SIZE), jnp.float32, -1.0 / np.sqrt(OUT_SIZE), 1.0 / np.sqrt(OUT_SIZE)), 'b2': jnp.zeros((OUT_SIZE,), jnp.float32)}
    _L1_gnn_all = _L1_gnn_setup()
    _L1_gnn_in = {k: v for k, v in _L1_gnn_all.items() if k in ('W_edge', 'b_edge', 'W1', 'b1', 'gamma', 'beta', 'W2', 'b2')}
    del _L1_gnn_all
    return {'x': x, 'src': src, 'dst': dst, 'edge_attr_16': edge_attr_16, 'L0_gnn_W0': _L0_gnn_in['W0'], 'L0_gnn_b0': _L0_gnn_in['b0'], 'L0_gnn_W1': _L0_gnn_in['W1'], 'L0_gnn_b1': _L0_gnn_in['b1'], 'L0_gnn_W2': _L0_gnn_in['W2'], 'L0_gnn_b2': _L0_gnn_in['b2'], 'L1_gnn_W_edge': _L1_gnn_in['W_edge'], 'L1_gnn_b_edge': _L1_gnn_in['b_edge'], 'L1_gnn_W1': _L1_gnn_in['W1'], 'L1_gnn_b1': _L1_gnn_in['b1'], 'L1_gnn_gamma': _L1_gnn_in['gamma'], 'L1_gnn_beta': _L1_gnn_in['beta'], 'L1_gnn_W2': _L1_gnn_in['W2'], 'L1_gnn_b2': _L1_gnn_in['b2']}

def reference(x, src, dst, edge_attr_16, L0_gnn_W0, L0_gnn_b0, L0_gnn_W1, L0_gnn_b1, L0_gnn_W2, L0_gnn_b2, L1_gnn_W_edge, L1_gnn_b_edge, L1_gnn_W1, L1_gnn_b1, L1_gnn_gamma, L1_gnn_beta, L1_gnn_W2, L1_gnn_b2):
    import jax
    import jax.numpy as jnp

    def _L0_gnn_ref(feat, W0, b0, W1, b1, W2, b2, src, dst):
        import jax, jax.numpy as jnp
        import numpy as np
        N_NODES = 12500
        N_EDGES = 150000
        D_IN = 64
        D_HID = 64

        def _norms(src, dst):
            ones = jnp.ones((src.shape[0],), jnp.float32)
            out_deg = jax.ops.segment_sum(ones, src, num_segments=N_NODES)
            in_deg = jax.ops.segment_sum(ones, dst, num_segments=N_NODES)
            out_norm = jax.lax.rsqrt(jnp.maximum(out_deg, 1.0))
            in_norm = jax.lax.rsqrt(jnp.maximum(in_deg, 1.0))
            return (out_norm, in_norm)

        def _graph_conv(x, src, dst, out_norm, in_norm, W, b):
            h = x * out_norm[:, None]
            agg = jax.ops.segment_sum(h[src], dst, num_segments=N_NODES)
            agg = agg * in_norm[:, None]
            return agg @ W + b
        out_norm, in_norm = _norms(src, dst)
        x = feat
        for W, b in ((W0, b0), (W1, b1), (W2, b2)):
            x = _graph_conv(x, src, dst, out_norm, in_norm, W, b)
            x = jax.nn.elu(x)
        return x

    def _L1_gnn_ref(x, edge_index, edge_attr, W_edge, b_edge, W1, b1, gamma, beta, W2, b2):
        import jax, jax.numpy as jnp
        import numpy as np
        N_NODES = 6250
        N_EDGES = 125000
        IN_SIZE = 64
        OUT_SIZE = 64
        EDGE_DIM = 16
        BN_EPS = 1e-05
        GIN_EPS = 0.0
        src = edge_index[0]
        dst = edge_index[1]
        ea = edge_attr @ W_edge.T + b_edge
        msg = jax.nn.relu(x[src] + ea)
        agg = jax.ops.segment_sum(msg, dst, num_segments=x.shape[0])
        h = (1.0 + GIN_EPS) * x + agg
        h = h @ W1.T + b1
        mean = jnp.mean(h, axis=0)
        var = jnp.var(h, axis=0)
        h = gamma * (h - mean) * jax.lax.rsqrt(var + BN_EPS) + beta
        h = jax.nn.relu(h)
        return h @ W2.T + b2
    edge_index = jnp.stack([src, dst])
    x = _layernorm(x + _L0_gnn_ref(x, L0_gnn_W0, L0_gnn_b0, L0_gnn_W1, L0_gnn_b1, L0_gnn_W2, L0_gnn_b2, src, dst), axis=-1)
    x = _layernorm(x + _L1_gnn_ref(x, edge_index, edge_attr_16, L1_gnn_W_edge, L1_gnn_b_edge, L1_gnn_W1, L1_gnn_b1, L1_gnn_gamma, L1_gnn_beta, L1_gnn_W2, L1_gnn_b2), axis=-1)
    return x

_drawn_inputs = setup_inputs


def setup_inputs(seed=0):
    import zlib

    import numpy as np

    out = dict(_drawn_inputs(seed))
    spreads = {'L0_gnn_b0': (0.0, 0.1),
     'L0_gnn_b1': (0.0, 0.1),
     'L0_gnn_b2': (0.0, 0.1),
     'L1_gnn_b_edge': (0.0, 0.1),
     'L1_gnn_b1': (0.0, 0.8),
     'L1_gnn_gamma': (1.0, 0.2),
     'L1_gnn_beta': (0.0, 0.1),
     'L1_gnn_b2': (0.0, 0.1)}
    factors = {'L0_gnn_W0': 7.188}
    for name, (base, spread) in spreads.items():
        noise = np.random.default_rng([zlib.crc32(name.encode()), seed]).standard_normal(out[name].shape)
        drawn = base * np.exp(spread * noise) if base else spread * noise
        out[name] = jnp.asarray(drawn.astype(out[name].dtype))
    for name, factor in factors.items():
        out[name] = (out[name] * factor).astype(out[name].dtype)
    return out
```

```python
import concourse.bass as bass
from concourse import mybir
from contextlib import ExitStack

F32 = mybir.dt.float32
BF16 = mybir.dt.bfloat16
F16 = mybir.dt.float16
I32 = mybir.dt.int32
ALU = mybir.AluOpType
ACT = mybir.ActivationFunctionType
AX = mybir.AxisListType

P = 128
NODES, EDGES, D, EDIM = 12500, 400000, 64, 16
LAYERS = 3
BLOCKS = -(-NODES // P)
FULL_BLOCKS = NODES // P
REST = NODES - FULL_BLOCKS * P
WIN = 512
WB = WIN // P
WINDOWS = -(-BLOCKS // WB)
PADDED = WINDOWS * WB
TILES = EDGES // P
UNIT = 5
GRAN = 2 * UNIT
GRANULES = -(-TILES // GRAN)
UNITS = TILES // UNIT
FOLD = 125
HIDDEN = 64 * 3
ROW = 256
LN_EPS, BN_EPS = 1e-5, 1e-5
BIG = 1.0e6


def gnn_kernel(nc, x, src, dst, dst_tiles, attr, w_l0, b_l0, w_edge, b_edge, w1, b1, gamma, beta,
               w2, b2, out):
    ctx = ExitStack()
    with ctx:
        def sb(name, shape, dt=F32):
            return ctx.enter_context(nc.sbuf_tensor(name, shape, dt))

        def pb(name, shape, dt=F32):
            return ctx.enter_context(nc.psum_tensor(name, shape, dt))

        def sem(name):
            return ctx.enter_context(nc.semaphore(name))

        table16 = nc.dram_tensor("table16", (BLOCKS * P, HIDDEN), BF16, kind="Internal").ap()
        table32 = nc.dram_tensor("table32", (BLOCKS * P, D), F32, kind="Internal").ap()
        extremes = nc.dram_tensor("extremes", (2, FOLD * (TILES // FOLD)), F32, kind="Internal").ap()

        src_key = sb("src_key", [P, GRANULES * GRAN], I32)
        dst_key = sb("dst_key", [P, GRANULES * GRAN])
        feat = sb("feat", [P, PADDED, D])
        hid = sb("hid", [P, PADDED, D + 1])
        tmp = sb("tmp", [P, PADDED, D])
        wide = sb("wide", [P, PADDED * P])
        parts = wide[:, 0:BLOCKS * HIDDEN // 2].bitcast(BF16).rearrange("p (b f) -> p b f", f=HIDDEN)
        hiddenT = wide[0:D, :]
        keys_i = wide[:, 0:GRANULES * GRAN].bitcast(I32)
        src_lo = wide[:, GRANULES * GRAN:2 * GRANULES * GRAN]
        src_hi = wide[:, 2 * GRANULES * GRAN:3 * GRANULES * GRAN]
        out_norm = sb("out_norm", [P, PADDED])
        in_norm = sb("in_norm", [P, PADDED])
        stat = sb("stat", [P, 4, PADDED])
        iota_win = sb("iota_win", [P, WIN], F16)
        win_base = sb("win_base", [P, WINDOWS])
        zeros16 = sb("zeros16", [P, WIN], BF16)
        ident = sb("ident", [P, P])
        idx = sb("idx", [P, 2, UNIT], I32)
        onehot = sb("onehot", [P, 2, UNIT, WIN], BF16)
        rows16 = sb("rows16", [P, 2, UNIT, ROW], BF16)
        rows32 = sb("rows32", [P, 2, UNIT, D])
        msg = sb("msg", [P, 2, UNIT, D])
        left = sb("left", [P, 2, UNIT, D])
        attr_sb = sb("attr_sb", [UNIT * EDIM, 2, P])
        w_edge_blk = sb("w_edge_blk", [UNIT * EDIM, UNIT, D])
        w_a = sb("w_a", [P, LAYERS, D + 1])
        w_b = sb("w_b", [P, LAYERS, D + 1])
        w1_a = sb("w1_a", [P, D])
        w2_sb = sb("w2_sb", [D, D])
        bias = sb("bias", [P, LAYERS + 2, D])
        cols = sb("cols", [D, 8])
        bn_st = sb("bn_st", [D, 25, 6])
        bn_mv = sb("bn_mv", [D, 2])
        agg_a = sb("agg_a", [P, WIN])
        agg_b = sb("agg_b", [P, WIN])
        feat_win = sb("feat_win", [P, WB, D])
        act_win = sb("act_win", [D, WIN])
        dst_fold_i = tmp[:, :, :].rearrange("p b f -> p (b f)")[0:FOLD, 0:TILES // FOLD * P].bitcast(I32)
        dst_fold = feat[:, :, :].rearrange("p b f -> p (b f)")[0:FOLD, 0:TILES // FOLD * P]
        ext = sb("ext", [FOLD, 2, TILES // FOLD])
        ext_all = hid[:, :, :].rearrange("p b f -> p (b f)")
        e_max = ext_all[0:WINDOWS, 0:GRANULES * GRAN]
        e_min = ext_all[0:WINDOWS, GRANULES * GRAN:2 * GRANULES * GRAN]
        g_ext = sb("g_ext", [WINDOWS, 4, GRANULES])
        iota_g = sb("iota_g", [WINDOWS, GRANULES])
        iota_i = sb("iota_i", [P, WIN], I32)
        edge_i = sb("edge_i", [WINDOWS, 1], I32)
        lims = sb("lims", [WINDOWS, 6])
        tri = sb("tri", [WINDOWS, WINDOWS + 1])
        bounds = sb("bounds", [1, WINDOWS, 4], I32)
        lo_hot = sb("lo_hot", [P, 2, UNIT, P], BF16)
        hi_hot = sb("hi_hot", [P, 2, UNIT, BLOCKS], BF16)

        acc_a = pb("acc_a", [P, WIN])
        acc_b = pb("acc_b", [P, WIN])
        node_ps = pb("node_ps", [P, WIN])
        edge_ps = [pb(f"edge_ps{s}", [P, WIN]) for s in range(2)]
        small_ps = pb("small_ps", [P, WIN])
        deg_ps = pb("deg_ps", [P, WIN])

        s_load = sem("s_load")
        s_keys = sem("s_keys")
        s_w = sem("s_w")
        s_iota = sem("s_iota")
        s_ext = sem("s_ext")
        s_extb = sem("s_extb")
        s_extw = sem("s_extw")
        s_tri = sem("s_tri")
        s_lims = sem("s_lims")
        s_bps = sem("s_bps")
        s_bounds = sem("s_bounds")
        s_hot = [sem(f"s_hot{s}") for s in range(2)]
        s_hist = [sem(f"s_hist{s}") for s in range(2)]
        s_deg = sem("s_deg")
        s_degc = sem("s_degc")
        s_sqrt = sem("s_sqrt")
        s_const = sem("s_const")
        s_chain = sem("s_chain")
        s_hi = sem("s_hi")
        s_parts = sem("s_parts")
        s_table = sem("s_table")
        s_x1 = sem("s_x1")
        s_exp_in = sem("s_exp_in")
        s_exp = sem("s_exp")
        s_ln_in = sem("s_ln_in")
        s_ln = sem("s_ln")
        s_bn = sem("s_bn")
        s_bnv = sem("s_bnv")
        s_bns = sem("s_bns")
        s_act = sem("s_act")
        s_mlp = sem("s_mlp")
        s_y = sem("s_y")
        s_final = sem("s_final")
        s_out = sem("s_out")
        s_memset = sem("s_memset")

        class EdgeSems:
            def __init__(self, n):
                self.idx = [sem(f"s_idx{n}_{s}") for s in range(2)]
                self.rows = [sem(f"s_rows{n}_{s}") for s in range(2)]
                self.read = [sem(f"s_read{n}_{s}") for s in range(2)]
                self.attr = [sem(f"s_attr{n}_{s}") for s in range(2)]
                self.hot = [sem(f"s_onehot{n}_{s}") for s in range(2)]
                self.sum = [sem(f"s_sum{n}_{s}") for s in range(2)]
                self.ea = [sem(f"s_ea{n}_{s}") for s in range(2)]
                self.msg = [sem(f"s_msg{n}_{s}") for s in range(2)]
                self.p1 = [sem(f"s_p1{n}_{s}") for s in range(2)]
                self.r1 = [sem(f"s_r1{n}_{s}") for s in range(2)]
                self.p2 = [sem(f"s_p2{n}_{s}") for s in range(2)]
                self.p3 = [sem(f"s_p3{n}_{s}") for s in range(2)]
                self.issue = sem(f"s_issue{n}")
                self.win = sem(f"s_win{n}")
                self.agg = sem(f"s_agg{n}")
                self.node = sem(f"s_node{n}")
                self.nodec = sem(f"s_nodec{n}")
                self.fwin = sem(f"s_fwin{n}")

        es = [EdgeSems(n) for n in range(LAYERS + 1)]
        GIN = LAYERS
        block = ctx.enter_context(nc.Block())

        def limits(engine, w):
            first = engine.value_load(bounds[0:1, bass.ds(w, 1), 0], min_val=0, max_val=WINDOWS * GRANULES)
            end = engine.value_load(bounds[0:1, bass.ds(w, 1), 1], min_val=1, max_val=WINDOWS * GRANULES)
            ahead = engine.value_load(bounds[0:1, bass.ds(w, 1), 2], min_val=0, max_val=WINDOWS * GRANULES)
            return first, end, ahead

        def granule(engine, j, ahead):
            return nc.s_assert_within(engine.snap(j - ahead), 0, GRANULES - 1, skip_runtime_bounds_check_because="bounds are clamped")


        @block.sync
        def _(sp):
            sp.dma_start(src_key[:, 0:TILES], src).then_inc(s_load, 16)
            sp.dma_start(keys_i[:, 0:TILES], dst).then_inc(s_load, 16)
            sp.dma_start(dst_fold_i, dst_tiles).then_inc(s_load, 16)
            sp.wait_ge(s_memset, 1)
            for n in range(LAYERS):
                for part in range(2):
                    sp.dma_start(w_a[part * D:(part + 1) * D, n, 0:D], w_l0[n]).then_inc(s_w, 16)
                sp.dma_start(w_b[0:D, n, 0:D], w_l0[n]).then_inc(s_w, 16)
                sp.dma_start(bias[:, n, :], b_l0[n].to_broadcast([P, D])).then_inc(s_w, 16)
            for part in range(2):
                sp.dma_start(w1_a[part * D:(part + 1) * D, :], w1).then_inc(s_w, 16)
            for k in range(UNIT):
                sp.dma_start(w_edge_blk[k * EDIM:(k + 1) * EDIM, k, :], w_edge).then_inc(s_w, 16)
            sp.dma_start(w2_sb[:, :], w2).then_inc(s_w, 16)
            sp.dma_start(bias[:, LAYERS, :], b_edge.to_broadcast([P, D])).then_inc(s_w, 16)
            sp.dma_start(bias[:, LAYERS + 1, :], b2.to_broadcast([P, D])).then_inc(s_w, 16)
            for n, v in enumerate((b1, gamma, beta)):
                sp.dma_start(cols[:, n:n + 1], v).then_inc(s_w, 16)
            sp.wait_ge(s_ext, 1)
            for n in range(2):
                sp.dma_start(extremes[n:n + 1, :].rearrange("o (p t) -> p (o t)", p=FOLD), ext[:, n, :]).then_inc(s_extb, 16)
            sp.wait_ge(s_extb, 32)
            sp.dma_start(e_max[:, 0:TILES], extremes[0:1, :].to_broadcast([WINDOWS, TILES])).then_inc(s_extw, 16)
            sp.dma_start(e_min[:, 0:TILES], extremes[1:2, :].to_broadcast([WINDOWS, TILES])).then_inc(s_extw, 16)
            sp.dma_start(feat[:, 0:FULL_BLOCKS, :], x[0:FULL_BLOCKS * P, :].rearrange("(b p) f -> p b f", p=P)).then_inc(s_x1, 16)
            sp.dma_start(feat[0:REST, FULL_BLOCKS, :], x[FULL_BLOCKS * P:NODES, :]).then_inc(s_x1, 16)
            sp.wait_ge(s_bounds, 1)
            for n in range(LAYERS + 1):
                sp.wait_ge(s_parts, n + 1)
                if n < LAYERS:
                    sp.dma_start(table16.rearrange("(b p) f -> p b f", p=P), parts[:, :, :]).then_inc(s_table, 16)
                else:
                    sp.dma_start(table32.rearrange("(b p) f -> p b f", p=P), tmp[:, 0:BLOCKS, :]).then_inc(s_table, 16)
                e = es[n]
                with sp.Fori(0, WINDOWS) as w:
                    first, end, ahead = limits(sp, w)
                    with sp.Fori(first, end) as j:
                        g = granule(sp, j, ahead)
                        for s in range(2):
                            sp.wait_ge(e.msg[s] if n == GIN else e.read[s], j + 1)
                            sp.dma_start(idx[:, s, :], src_key[:, bass.ds(g * GRAN + s * UNIT, UNIT)]).then_inc(e.idx[s], 16)
                            if n == GIN:
                                sp.wait_ge(e.ea[s], j + 1)
                                u = g * 2 + s
                                if s == 1:
                                    u = u - u // UNITS
                                u = nc.s_assert_within(u, 0, UNITS - 1, skip_runtime_bounds_check_because="bounds are clamped")
                                sp.dma_start(attr_sb[:, s, :], attr[bass.ds(u, 1), :, :].rearrange("u k p -> (u k) p")).then_inc(e.attr[s], 16)
            sp.wait_ge(s_final, 1)
            sp.dma_start(out[0:FULL_BLOCKS * P, :].rearrange("(b p) f -> p b f", p=P), feat[:, 0:FULL_BLOCKS, :]).then_inc(s_out, 16)
            sp.dma_start(out[FULL_BLOCKS * P:NODES, :], feat[0:REST, FULL_BLOCKS, :]).then_inc(s_out, 16)
            sp.wait_ge(s_out, 32)

        @block.gpsimd
        def _(pool):
            nc.gpsimd.iota(iota_i[:, :], [[1, WIN]], base=0, channel_multiplier=0).then_inc(s_iota, 1)
            nc.gpsimd.iota(edge_i[:, :], [[0, 1]], base=0, channel_multiplier=WIN).then_inc(s_iota, 1)
            nc.gpsimd.memset(ident[:, :], 0.0).then_inc(s_tri, 1)
            nc.gpsimd.memset(tri[:, :], 1.0).then_inc(s_tri, 1)
            pool.wait_ge(s_tri, 2)
            nc.gpsimd.affine_select(out=ident[:, :], in_=ident[:, :], pattern=[[-1, P]], compare_op=ALU.not_equal,
                                    fill=1.0, base=0, channel_multiplier=1).then_inc(s_tri, 1)
            nc.gpsimd.affine_select(out=tri[:, :], in_=tri[:, :], pattern=[[1, WINDOWS + 1]], compare_op=ALU.is_gt,
                                    fill=0.0, base=0, channel_multiplier=-1).then_inc(s_tri, 1)
            pool.wait_ge(s_bounds, 1)
            for n in range(LAYERS + 1):
                e = es[n]
                pool.wait_ge(s_table, 16 * (n + 1))
                with pool.Fori(0, WINDOWS) as w:
                    first, end, ahead = limits(pool, w)
                    with pool.Fori(first, end) as j:
                        for s in range(2):
                            pool.wait_ge(e.idx[s], (j + 1) * 16)
                            pool.wait_ge(e.msg[s] if n == GIN else e.sum[s], j + 1)
                            pool.sem_inc(e.issue, 1)
                            for k in range(UNIT):
                                nc.gpsimd.indirect_dma_start(
                                    out=rows32[:, s, k, :] if n == GIN else rows16[:, s, k, 0:HIDDEN], out_offset=None,
                                    in_=(table32 if n == GIN else table16)[:, :],
                                    in_offset=bass.IndirectOffsetOnAxis(ap=idx[:, s, k:k + 1], axis=0),
                                ).then_inc(e.rows[s], 16)

        @block.vector
        def _(dve):
            for c in (es[GIN].msg[0], es[GIN].msg[1], es[GIN].p3[0], es[GIN].p3[1], s_y):
                dve.sem_inc(c, 1)
            count = [0]

            def link(ins):
                count[0] += 1
                ins.then_inc(s_chain, 1)
                dve.wait_ge(s_chain, count[0])

            V = nc.vector
            V.memset(w_a[:, :, :], 0.0)
            V.memset(w_edge_blk[:, :, :], 0.0)
            V.memset(bounds[:, :, :], 0)
            V.memset(src_key[:, TILES:], 0)
            V.memset(zeros16[:, :], 0.0)
            V.memset(feat[:, FULL_BLOCKS:, :], 0.0)
            V.memset(rows16[:, :, :, HIDDEN + 1:], 0.0)
            V.memset(rows16[:, :, :, HIDDEN:HIDDEN + 1], 1.0)
            link(V.memset(w_b[:, :, :], 0.0))
            V.memset(w_b[D:D + 1, :, D:D + 1], 1.0).then_inc(s_memset, 1)
            dve.wait_ge(s_memset, 1)
            dve.wait_ge(s_iota, 2)
            V.tensor_copy(iota_g[:, :], iota_i[0:WINDOWS, 0:GRANULES])
            V.tensor_copy(lims[:, 0:1], edge_i[:, :])
            link(V.tensor_copy(iota_win[:, :], iota_i[:, :]))
            link(V.tensor_scalar(win_base[:, :], iota_win[:, 0:WINDOWS], float(WIN), None, ALU.mult))
            link(V.tensor_scalar(lims[:, 1:2], lims[:, 0:1], float(WIN), None, ALU.add))
            dve.wait_ge(s_load, 48)
            V.memset(dst_key[:, TILES:], -1.0)
            V.tensor_copy(dst_key[:, 0:TILES], keys_i[:, 0:TILES])
            link(V.tensor_copy(dst_fold, dst_fold_i))
            fold3 = dst_fold.rearrange("p (t e) -> p t e", e=P)
            V.tensor_reduce(ext[:, 0, :], fold3, axis=AX.X, op=ALU.max)
            V.tensor_reduce(ext[:, 1, :], fold3, axis=AX.X, op=ALU.min).then_inc(s_ext, 1)
            V.tensor_scalar(keys_i, src_key[:, :], P.bit_length() - 1, None, ALU.logical_shift_right)
            link(V.tensor_scalar(tmp[:, :, :].rearrange("p b f -> p (b f)")[:, 0:GRANULES * GRAN].bitcast(I32), src_key[:, :], P - 1, None, ALU.bitwise_and))
            V.tensor_copy(src_hi, keys_i)
            link(V.tensor_copy(src_lo, tmp[:, :, :].rearrange("p b f -> p (b f)")[:, 0:GRANULES * GRAN].bitcast(I32)))
            link(V.memset(src_hi[:, TILES:], -1.0))
            V.memset(e_max[:, TILES:], -1.0)
            link(V.memset(e_min[:, TILES:], BIG))
            dve.wait_ge(s_extw, 32)
            V.tensor_reduce(g_ext[:, 0, :], e_max.rearrange("p (g t) -> p g t", t=GRAN), axis=AX.X, op=ALU.max)
            link(V.tensor_reduce(g_ext[:, 1, :], e_min.rearrange("p (g t) -> p g t", t=GRAN), axis=AX.X, op=ALU.min))
            link(V.tensor_scalar(g_ext[:, 2, :], g_ext[:, 0, :], lims[:, 0:1], BIG, ALU.is_lt, ALU.mult))
            link(V.tensor_tensor(g_ext[:, 0, :], g_ext[:, 2, :], iota_g[:, :], ALU.add))
            link(V.tensor_reduce(lims[:, 2:3], g_ext[:, 0, :], axis=AX.X, op=ALU.min))
            link(V.tensor_scalar(g_ext[:, 2, :], g_ext[:, 1, :], lims[:, 1:2], None, ALU.is_lt))
            link(V.tensor_scalar(g_ext[:, 3, :], iota_g[:, :], 1.0, None, ALU.add))
            link(V.tensor_tensor(g_ext[:, 1, :], g_ext[:, 2, :], g_ext[:, 3, :], ALU.mult))
            link(V.tensor_reduce(lims[:, 3:4], g_ext[:, 1, :], axis=AX.X, op=ALU.max))
            link(V.tensor_scalar(lims[:, 2:3], lims[:, 2:3], float(GRANULES - 1), None, ALU.min))
            link(V.tensor_tensor(lims[:, 4:5], lims[:, 3:4], lims[:, 2:3], ALU.subtract))
            link(V.tensor_scalar(lims[:, 4:5], lims[:, 4:5], 1.0, None, ALU.max))
            V.tensor_scalar(lims[:, 5:6], lims[:, 2:3], -1.0, None, ALU.mult).then_inc(s_lims, 1)
            dve.wait_ge(s_bps, 1)
            V.tensor_copy(bounds[:, :, 0], small_ps[0:1, 0:WINDOWS])
            V.tensor_copy(bounds[:, :, 1], small_ps[0:1, 1:WINDOWS + 1])
            V.tensor_copy(bounds[:, :, 2], small_ps[0:1, 32:32 + WINDOWS]).then_inc(s_bounds, 1)
            with V.Fori(0, GRANULES) as g:
                for s in range(2):
                    dve.wait_ge(s_hist[s], g + 1)
                    for k in range(UNIT):
                        t = g * GRAN + s * UNIT + k
                        V.tensor_scalar(lo_hot[:, s, k, :], iota_win[:, 0:P], src_lo[:, bass.ds(t, 1)], None, ALU.is_equal)
                        last = V.tensor_scalar(hi_hot[:, s, k, :], iota_win[:, 0:BLOCKS], src_hi[:, bass.ds(t, 1)], None, ALU.is_equal)
                    last.then_inc(s_hot[s], 1)
            dve.wait_ge(s_deg, 1)
            V.tensor_scalar(stat[:, 0, 0:BLOCKS], deg_ps[:, 0:BLOCKS], 1.0, None, ALU.max).then_inc(s_degc, 1)
            dve.wait_ge(s_sqrt, 1)
            link(V.reciprocal(out_norm[:, 0:BLOCKS], stat[:, 1, 0:BLOCKS]))
            dve.wait_ge(s_x1, 32)

            def over(vec):
                return vec[:, 0:BLOCKS].rearrange("p (b o) -> p b o", o=1).to_broadcast([P, BLOCKS, D])

            def row(n):
                return bias[:, n:n + 1, :].to_broadcast([P, BLOCKS, D])

            T, H, X = tmp[:, 0:BLOCKS, :], hid[:, 0:BLOCKS, 0:D], feat[:, 0:BLOCKS, :]

            def split(n):
                link(V.tensor_copy(parts[:, :, 0:D], T))
                link(V.tensor_tensor(T, T, parts[:, :, 0:D], ALU.subtract))
                link(V.tensor_copy(parts[:, :, D:2 * D], T))
                V.tensor_tensor(parts[:, :, 2 * D:3 * D], T, parts[:, :, D:2 * D], ALU.subtract).then_inc(s_parts, 1)

            def layer_norm(n):
                link(V.tensor_reduce(stat[:, 0, 0:BLOCKS], X, axis=AX.X, op=ALU.add))
                link(V.tensor_scalar(stat[:, 0, 0:BLOCKS], stat[:, 0, 0:BLOCKS], 1.0 / D, None, ALU.mult))
                link(V.tensor_tensor(X, X, over(stat[:, 0, :]), ALU.subtract))
                link(V.tensor_tensor(T, X, X, ALU.mult))
                link(V.tensor_reduce(stat[:, 1, 0:BLOCKS], T, axis=AX.X, op=ALU.add))
                V.tensor_scalar(stat[:, 2, 0:BLOCKS], stat[:, 1, 0:BLOCKS], 1.0 / D, LN_EPS, ALU.mult, ALU.add).then_inc(s_ln_in, 1)
                dve.wait_ge(s_ln, n + 1)
                link(V.reciprocal(stat[:, 3, 0:BLOCKS], stat[:, 0, 0:BLOCKS]))

            link(V.tensor_tensor(T, X, over(out_norm), ALU.mult))
            split(0)
            dve.wait_ge(s_w, 16 * (4 * LAYERS + 2 + UNIT + 6))
            for n in range(LAYERS + 1):
                e = es[n]
                with V.Fori(0, WINDOWS) as w:
                    first, end, ahead = limits(V, w)
                    with V.Fori(first, end) as j:
                        g = granule(V, j, ahead)
                        for s in range(2):
                            def hot(k):
                                return V.tensor_scalar(onehot[:, s, k, :], iota_win[:, :], win_base[:, bass.ds(w, 1)],
                                                       dst_key[:, bass.ds(g * GRAN + s * UNIT + k, 1)], ALU.add, ALU.is_equal)
                            if n == GIN:
                                dve.wait_ge(e.rows[s], (j + 1) * (16 * UNIT))
                                dve.wait_ge(e.ea[s], j + 2)
                                dve.wait_ge(e.p3[s], j + 1)
                                V.tensor_tensor(msg[:, s, :, :], edge_ps[s][:, 0:UNIT * D].rearrange("p (k f) -> p k f", f=D),
                                                rows32[:, s, :, :], ALU.add).then_inc(e.msg[s], 1)
                            dve.wait_ge(e.sum[s], j + 1)
                            for k in range(UNIT):
                                last = hot(k)
                            last.then_inc(e.hot[s], 1)
                            if n == GIN:
                                dve.wait_ge(e.p1[s], j + 1)
                                V.scalar_tensor_tensor(out=left[:, s, :, :], in0=msg[:, s, :, :], scalar=0.0, in1=rows16[:, s, :, 0:D],
                                                       op0=ALU.max, op1=ALU.subtract).then_inc(e.r1[s], 1)
                                dve.wait_ge(e.p2[s], j + 1)
                                V.tensor_tensor(rows16[:, s, :, 2 * D:3 * D], left[:, s, :, :], rows16[:, s, :, D:2 * D],
                                                ALU.subtract).then_inc(e.p3[s], 1)
                if n == GIN:
                    break
                dve.wait_ge(e.nodec, WINDOWS + 1)
                if n == 0:
                    V.tensor_scalar(stat[:, 0, 0:BLOCKS], hid[:, 0:BLOCKS, D], 1.0, None, ALU.max).then_inc(s_degc, 1)
                    dve.wait_ge(s_sqrt, 2)
                    link(V.reciprocal(in_norm[:, 0:BLOCKS], stat[:, 1, 0:BLOCKS]))
                link(V.tensor_tensor(H, H, over(in_norm), ALU.mult))
                link(V.tensor_tensor(H, H, row(n), ALU.add))
                V.tensor_scalar(T, H, 0.0, None, ALU.min).then_inc(s_exp_in, 1)
                dve.wait_ge(s_exp, n + 1)
                link(V.tensor_scalar(H, H, 0.0, None, ALU.max))
                if n < LAYERS - 1:
                    link(V.scalar_tensor_tensor(out=T, in0=T, scalar=-1.0, in1=H, op0=ALU.add, op1=ALU.add))
                    link(V.tensor_tensor(T, T, over(out_norm), ALU.mult))
                    dve.wait_ge(s_table, 16 * (n + 1))
                    split(n + 1)
                else:
                    link(V.scalar_tensor_tensor(out=T, in0=T, scalar=-1.0, in1=H, op0=ALU.add, op1=ALU.add))
                    link(V.tensor_tensor(X, X, T, ALU.add))
                    layer_norm(0)
                    link(V.tensor_tensor(X, X, over(stat[:, 3, :]), ALU.mult))
                    V.tensor_tensor(T, X, row(LAYERS), ALU.add).then_inc(s_parts, 1)
            dve.wait_ge(es[GIN].nodec, WINDOWS + 1)
            for c in range(NODES // 500):
                last = V.bn_stats(bn_st[:, c, :], hiddenT[:, c * 500:(c + 1) * 500])
            link(last)
            link(V.bn_aggr(bn_mv[:, :], bn_st[:, :, :].rearrange("p c s -> p (c s)")))
            V.tensor_scalar(cols[:, 3:4], bn_mv[:, 1:2], BN_EPS, None, ALU.add).then_inc(s_bnv, 1)
            dve.wait_ge(s_bns, 1)
            link(V.reciprocal(cols[:, 5:6], cols[:, 4:5]))
            link(V.tensor_tensor(cols[:, 6:7], cols[:, 5:6], cols[:, 1:2], ALU.mult))
            link(V.tensor_tensor(cols[:, 5:6], cols[:, 6:7], bn_mv[:, 0:1], ALU.mult))
            V.tensor_tensor(cols[:, 7:8], cols[:, 2:3], cols[:, 5:6], ALU.subtract).then_inc(s_bn, 1)
            with V.Fori(0, WINDOWS) as w:
                dve.wait_ge(s_mlp, w + 2)
                V.tensor_tensor(hid[:, bass.ds(w * WB, WB), 0:D], node_ps[:, 0:WB * D].rearrange("p (b f) -> p b f", f=D),
                                feat[:, bass.ds(w * WB, WB), :], ALU.add).then_inc(s_y, 1)
            dve.wait_ge(s_y, WINDOWS + 1)
            link(V.tensor_tensor(X, H, row(LAYERS + 1), ALU.add))
            layer_norm(1)
            V.tensor_tensor(X, X, over(stat[:, 3, :]), ALU.mult).then_inc(s_final, 1)

        @block.scalar
        def _(act):
            A = nc.scalar
            for n in range(LAYERS + 1):
                for c in (es[n].agg, es[n].nodec) + (() if n == GIN else (es[n].read[0], es[n].read[1])):
                    act.sem_inc(c, 1)

            def node_windows(n, e):
                with A.Fori(0, WINDOWS) as w:
                    if n == GIN:
                        act.wait_ge(e.node, w + 1)
                        A.copy(feat_win[:, :, :], feat[:, bass.ds(w * WB, WB), :]).then_inc(e.fwin, 1)
                    first, end, ahead = limits(A, w)
                    with A.Fori(first, end) as j:
                        for s in range(2):
                            if n < GIN:
                                act.wait_ge(e.rows[s], (j + 1) * (16 * UNIT))
                                act.sem_inc(e.read[s], 1)
                            else:
                                act.wait_ge(e.msg[s], j + 2)
                                act.wait_ge(e.sum[s], j + 1)
                                A.activation(rows16[:, s, :, 0:D], msg[:, s, :, :], ACT.Relu).then_inc(e.p1[s], 1)
                                act.wait_ge(e.r1[s], j + 1)
                                A.copy(rows16[:, s, :, D:2 * D], left[:, s, :, :]).then_inc(e.p2[s], 1)
                    act.wait_ge(e.win, w + 1)
                    act.wait_ge(e.node, w + 1)
                    A.copy(agg_a[:, :], acc_a[:, :])
                    A.copy(agg_b[:, :], acc_b[:, :]).then_inc(e.agg, 1)
                    act.wait_ge(e.node, w + 2)
                    if n == GIN:
                        A.activation(hiddenT[:, bass.ds(w * WIN, WIN)], node_ps[0:D, :], ACT.Identity,
                                     bias=cols[:, 0:1]).then_inc(e.nodec, 1)
                    else:
                        A.copy(hid[:, bass.ds(w * WB, WB), :], node_ps[:, 0:WB * (D + 1)].rearrange("p (b f) -> p b f", f=D + 1)).then_inc(e.nodec, 1)

            act.wait_ge(s_bounds, 1)
            act.wait_ge(s_degc, 1)
            A.activation(stat[:, 1, 0:BLOCKS], stat[:, 0, 0:BLOCKS], ACT.Sqrt).then_inc(s_sqrt, 1)
            for n in range(LAYERS):
                node_windows(n, es[n])
                if n == 0:
                    act.wait_ge(s_degc, 2)
                    A.activation(stat[:, 1, 0:BLOCKS], stat[:, 0, 0:BLOCKS], ACT.Sqrt).then_inc(s_sqrt, 1)
                act.wait_ge(s_exp_in, n + 1)
                A.activation(tmp[:, 0:BLOCKS, :], tmp[:, 0:BLOCKS, :], ACT.Exp).then_inc(s_exp, 1)
            act.wait_ge(s_ln_in, 1)
            A.activation(stat[:, 0, 0:BLOCKS], stat[:, 2, 0:BLOCKS], ACT.Sqrt).then_inc(s_ln, 1)
            act.wait_ge(s_table, 16 * (LAYERS + 1))
            node_windows(GIN, es[GIN])
            act.wait_ge(s_bnv, 1)
            A.activation(cols[:, 4:5], cols[:, 3:4], ACT.Sqrt).then_inc(s_bns, 1)
            act.wait_ge(s_bn, 1)
            with A.Fori(0, WINDOWS) as w:
                act.wait_ge(s_mlp, w + 1)
                A.activation(act_win[:, :], hiddenT[:, bass.ds(w * WIN, WIN)], ACT.Relu, bias=cols[:, 7:8],
                             scale=cols[:, 6:7]).then_inc(s_act, 1)
            act.wait_ge(s_ln_in, 2)
            A.activation(stat[:, 0, 0:BLOCKS], stat[:, 2, 0:BLOCKS], ACT.Sqrt).then_inc(s_ln, 1)

        @block.tensor
        def _(pe):
            M = nc.tensor.matmul
            for c in (s_hist[0], s_hist[1], es[GIN].ea[0], es[GIN].ea[1], s_mlp):
                pe.sem_inc(c, 1)
            for n in range(LAYERS + 1):
                for c in (es[n].sum[0], es[n].sum[1], es[n].node):
                    pe.sem_inc(c, 1)
            pe.wait_ge(s_lims, 1)
            pe.wait_ge(s_tri, 4)
            M(small_ps[0:1, 0:WINDOWS + 1], lims[:, 4:5], tri[:, :], start=True, stop=True)
            M(small_ps[0:1, 32:32 + WINDOWS], lims[:, 4:5], tri[:, 0:WINDOWS], start=True, stop=False)
            M(small_ps[0:1, 32:32 + WINDOWS], lims[:, 5:6], ident[0:WINDOWS, 0:WINDOWS], start=False, stop=True).then_inc(s_bps, 1)
            M(deg_ps[:, 0:BLOCKS], zeros16[:, 0:P], zeros16[:, 0:BLOCKS], start=True, stop=False)
            with nc.tensor.Fori(0, GRANULES) as g:
                for s in range(2):
                    pe.wait_ge(s_hot[s], g + 1)
                    for k in range(UNIT):
                        last = M(deg_ps[:, 0:BLOCKS], lo_hot[:, s, k, :], hi_hot[:, s, k, :], start=False, stop=False)
                    last.then_inc(s_hist[s], 1)
            M(deg_ps[:, 0:BLOCKS], zeros16[:, 0:P], zeros16[:, 0:BLOCKS], start=False, stop=True).then_inc(s_deg, 1)
            pe.wait_ge(s_bounds, 1)
            pe.wait_ge(s_w, 16 * (4 * LAYERS + 2 + UNIT + 6))
            for n in range(LAYERS + 1):
                e = es[n]
                with nc.tensor.Fori(0, WINDOWS) as w:
                    first, end, ahead = limits(nc.tensor, w)
                    pe.wait_ge(e.agg, w + 1)
                    M(acc_a[:, :], zeros16[:, 0:P], zeros16[:, :], start=True, stop=False)
                    M(acc_b[:, :], zeros16[:, 0:P], zeros16[:, :], start=True, stop=False)
                    if n == GIN:
                        pe.wait_ge(e.fwin, w + 1)
                        for c in range(WB):
                            M(acc_b[0:D, c * P:(c + 1) * P], feat_win[:, c, :], ident[:, :], start=False, stop=False)
                    with nc.tensor.Fori(first, end) as j:
                        if n == GIN:
                            for s in range(2):
                                pe.wait_ge(e.attr[s], (j + 1) * 16)
                                pe.wait_ge(e.msg[s], j + 1)
                                M(edge_ps[s][:, 0:UNIT * D], attr_sb[:, s, :], w_edge_blk[:, :, :].rearrange("p k f -> p (k f)"),
                                  start=True, stop=True).then_inc(e.ea[s], 1)
                        for s in range(2):
                            pe.wait_ge(e.hot[s], j + 1)
                            if n == GIN:
                                pe.wait_ge(e.p3[s], j + 2)
                            else:
                                pe.wait_ge(e.rows[s], (j + 1) * (16 * UNIT))
                            for k in range(UNIT):
                                M(acc_a[:, :], rows16[:, s, k, 0:P], onehot[:, s, k, :], start=False, stop=False)
                                last = M(acc_b[:, :], rows16[:, s, k, P:2 * P], onehot[:, s, k, :], start=False, stop=False)
                            last.then_inc(e.sum[s], 1)
                    M(acc_a[:, :], zeros16[:, 0:P], zeros16[:, :], start=False, stop=True)
                    M(acc_b[:, :], zeros16[:, 0:P], zeros16[:, :], start=False, stop=True).then_inc(e.win, 1)
                    pe.wait_ge(e.agg, w + 2)
                    pe.wait_ge(e.nodec, w + 1)
                    if n == GIN:
                        M(node_ps[0:D, :], w1_a[:, :], agg_a[:, :], start=True, stop=False)
                        M(node_ps[0:D, :], w1_a[0:D, :], agg_b[0:D, :], start=False, stop=True).then_inc(e.node, 1)
                    else:
                        for c in range(WB):
                            o = node_ps[:, c * (D + 1):(c + 1) * (D + 1)]
                            M(o, agg_a[:, c * P:(c + 1) * P], w_a[:, n, :], start=True, stop=False)
                            last = M(o, agg_b[:, c * P:(c + 1) * P], w_b[:, n, :], start=False, stop=True)
                        last.then_inc(e.node, 1)
            pe.wait_ge(es[GIN].nodec, WINDOWS + 1)
            with nc.tensor.Fori(0, WINDOWS) as w:
                pe.wait_ge(s_act, w + 1)
                pe.wait_ge(s_y, w + 1)
                for c in range(WB):
                    last = M(node_ps[:, c * D:(c + 1) * D], act_win[:, c * P:(c + 1) * P], w2_sb[:, :], start=True, stop=True)
                last.then_inc(s_mlp, 1)


def kernel(x, src, dst, edge_attr_16, L0_gnn_W0, L0_gnn_b0, L0_gnn_W1, L0_gnn_b1, L0_gnn_W2, L0_gnn_b2,
           L1_gnn_W_edge, L1_gnn_b_edge, L1_gnn_W1, L1_gnn_b1, L1_gnn_gamma, L1_gnn_beta, L1_gnn_W2, L1_gnn_b2):
    import numpy as np
    import concourse.bacc as bacc
    from concourse.bass_utils import run_bass_kernel_spmd

    laid_out = {
        "x": np.asarray(x),
        "src": np.asarray(src).reshape(TILES, P).T,
        "dst": np.asarray(dst).reshape(TILES, P).T,
        "dst_tiles": np.asarray(dst).reshape(FOLD, TILES // FOLD * P),
        "attr": np.asarray(edge_attr_16).reshape(UNITS, UNIT, P, EDIM).transpose(0, 1, 3, 2).reshape(UNITS, UNIT * EDIM, P),
        "w_l0": np.stack([np.asarray(w) for w in (L0_gnn_W0, L0_gnn_W1, L0_gnn_W2)]),
        "b_l0": np.stack([np.asarray(b) for b in (L0_gnn_b0, L0_gnn_b1, L0_gnn_b2)]).reshape(LAYERS, 1, D),
        "w_edge": np.asarray(L1_gnn_W_edge).T,
        "b_edge": np.asarray(L1_gnn_b_edge).reshape(1, D),
        "w1": np.asarray(L1_gnn_W1).T,
        "b1": np.asarray(L1_gnn_b1).reshape(D, 1),
        "gamma": np.asarray(L1_gnn_gamma).reshape(D, 1),
        "beta": np.asarray(L1_gnn_beta).reshape(D, 1),
        "w2": np.asarray(L1_gnn_W2).T,
        "b2": np.asarray(L1_gnn_b2).reshape(1, D),
    }
    nc = bacc.Bacc("TRN2", target_bir_lowering=False, num_devices=1)
    arrays = {f"{name}_dram": np.ascontiguousarray(a) for name, a in laid_out.items()}
    args = [nc.dram_tensor(name, a.shape, mybir.dt.from_np(a.dtype), kind="ExternalInput").ap() for name, a in arrays.items()]
    out = nc.dram_tensor("out_dram", (NODES, D), F32, kind="ExternalOutput").ap()
    gnn_kernel(nc, *args, out)
    return run_bass_kernel_spmd(nc, [arrays], core_ids=[0]).results[0]["out_dram"]
```

```python
import concourse.bass as bass
from concourse import mybir
from contextlib import ExitStack

F32 = mybir.dt.float32
BF16 = mybir.dt.bfloat16
F16 = mybir.dt.float16
F8 = mybir.dt.float8e4
I32 = mybir.dt.int32
U16 = mybir.dt.uint16
ALU = mybir.AluOpType
ACT = mybir.ActivationFunctionType
AX = mybir.AxisListType

P = 128
NODES, EDGES, D, EDIM = 12500, 400000, 64, 16
LAYERS = 3
BLOCKS = -(-NODES // P)
FULL_BLOCKS = NODES // P
REST = NODES - FULL_BLOCKS * P
WIN = 512
WB = WIN // P
WINDOWS = -(-BLOCKS // WB)
PADDED = WINDOWS * WB
TILES = EDGES // P
UNIT = 5
GRAN = 2 * UNIT
GRANULES = -(-TILES // GRAN)
UNITS = TILES // UNIT
FOLD = 125
HIDDEN = 64 * 3
ROW = 256
LN_EPS, BN_EPS = 1e-5, 1e-5
BIG = 1.0e6
GROUP = 8
HALF_BANK = BLOCKS // 2 * GROUP
GCOLS = BLOCKS * GROUP
HALF = WIN // 2
GPH = HALF // GROUP
GPW = 2 * GPH
GROUPS = WINDOWS * GPW
DENSE = 3
OTHERS = 2
SLOTS = 2 * DENSE + OTHERS
SHIFT = 4096
PIECES = 7
PB = BLOCKS // PIECES
UNIT_COUNT = 16.0
LO_SCALE = 2048.0


def gnn_kernel(nc, x, src, dst, dst_tiles, dst_back, attr, w_l0, b_l0, w_edge, b_edge, w1, b1, gamma, beta,
               w2, b2, out):
    ctx = ExitStack()
    with ctx:
        def sb(name, shape, dt=F32):
            return ctx.enter_context(nc.sbuf_tensor(name, shape, dt))

        def pb(name, shape, dt=F32):
            return ctx.enter_context(nc.psum_tensor(name, shape, dt))

        def sem(name):
            return ctx.enter_context(nc.semaphore(name))

        table16 = nc.dram_tensor("table16", (BLOCKS * P, HIDDEN), BF16, kind="Internal").ap()
        table32 = nc.dram_tensor("table32", (BLOCKS * P, D), F32, kind="Internal").ap()
        extremes = nc.dram_tensor("extremes", (2, FOLD * (TILES // FOLD)), F32, kind="Internal").ap()
        running = nc.dram_tensor("running", (2, TILES), F32, kind="Internal").ap()
        degrees = nc.dram_tensor("degrees", (WINDOWS, GPW, GROUP), F32, kind="Internal").ap()
        counts = nc.dram_tensor("counts", (WINDOWS, 2, P, BLOCKS * HALF // 4), I32, kind="Internal").ap()

        src_key = sb("src_key", [P, GRANULES * GRAN], I32)
        dst_key = sb("dst_key", [P, GRANULES * GRAN])
        feat = sb("feat", [P, PADDED, D])
        hid = sb("hid", [P, PADDED, D + 1])
        tmp = sb("tmp", [P, PADDED, D])
        wide = sb("wide", [P, PADDED * P])
        parts = wide[:, 0:BLOCKS * HIDDEN // 2].bitcast(BF16).rearrange("p (b f) -> p b f", f=HIDDEN)
        hiddenT = wide[0:D, :]
        KEYS = GRANULES * GRAN
        tmp_row = tmp[:, :, :].rearrange("p b f -> p (b f)")
        hid_row = hid[:, :, :].rearrange("p b f -> p (b f)")
        keys_i = wide[:, 0:KEYS].bitcast(I32)
        digit_i = wide[:, KEYS:2 * KEYS].bitcast(I32)
        pair_key = hid_row[:, 0:KEYS]
        src_lo = hid_row[:, KEYS:2 * KEYS]
        src_hi = tmp_row[:, 0:KEYS]
        group_word = tmp_row[0:1, 0:GROUPS // 2].bitcast(I32)
        group_flags = tmp_row[0:1, GROUPS // 2:GROUPS].bitcast(I32)
        group_p = tmp_row[0:1, GROUPS:2 * GROUPS + 1].bitcast(I32)
        group_d = tmp_row[0:1, 2 * GROUPS + 1:3 * GROUPS + 1].bitcast(I32)
        win_words = [wide[:, h * (BLOCKS * HALF // 4):(h + 1) * (BLOCKS * HALF // 4)].bitcast(I32) for h in range(2)]
        win_pairs = [w.bitcast(U16) for w in win_words]
        piece_words = wide[:, 0:BLOCKS * WIN // 4].bitcast(I32).rearrange("p (k h n) -> p k h n", k=PIECES, h=2)
        pieces = wide[:, 0:BLOCKS * WIN // 4].bitcast(F8).rearrange("p (k h n) -> p k h n", k=PIECES, h=2)
        rows_f16 = sb("rows_f16", [P, BLOCKS, P], F16)
        spare = rows_f16[:, :, :].rearrange("p b f -> p (b f)")
        SP_LO = SLOTS * GCOLS
        SP_IOTA = SP_LO + SLOTS * P
        SP_BASE = SP_IOTA + GCOLS
        key_hot = spare[:, 0:SP_LO].rearrange("p (r c) -> p r c", r=SLOTS)
        lo_ring = spare[:, SP_LO:SP_IOTA].rearrange("p (r c) -> p r c", r=SLOTS)
        hi_hot = spare[:, 0:2 * UNIT * BLOCKS].rearrange("p (s k c) -> p s k c", s=2, k=UNIT)
        iota_key = spare[:, SP_IOTA:SP_BASE]
        group_base = spare[:, SP_BASE:SP_BASE + 2 * GROUPS].bitcast(F32)
        ROWS = 2 * UNIT * D
        rows32, msg, left = (spare[:, 2 * n * ROWS:2 * (n + 1) * ROWS].bitcast(F32).rearrange("p (s k f) -> p s k f", s=2, k=UNIT)
                             for n in range(3))
        act_win = spare[0:D, 6 * ROWS:6 * ROWS + 2 * WIN].bitcast(F32)
        FW = 6 * ROWS + 2 * WIN
        feat_win = spare[:, FW:FW + 2 * WB * D].bitcast(F32).rearrange("p (b f) -> p b f", f=D)
        attr_sb = spare[0:UNIT * EDIM, FW + 2 * WB * D:FW + 2 * WB * D + 4 * P].bitcast(F32).rearrange("p (s e) -> p s e", s=2)
        row_buf = wide[0:1, 2 * KEYS:2 * KEYS + 2 * TILES].rearrange("p (n t) -> p n t", n=2)
        count_row = feat[:, :, :].rearrange("p b f -> p (b f)")[0:1, 0:4 * GROUPS].rearrange("p (n g) -> p n g", n=4)
        out_norm = sb("out_norm", [P, PADDED])
        in_norm = sb("in_norm", [P, PADDED])
        stat = sb("stat", [P, 4, PADDED])
        iota_win = sb("iota_win", [P, WIN], F16)
        win_base = sb("win_base", [P, WINDOWS])
        zeros16 = sb("zeros16", [P, WIN], BF16)
        ident = sb("ident", [P, P])
        idx = sb("idx", [P, 2, UNIT], I32)
        onehot = sb("onehot", [P, 2, UNIT, WIN], BF16)
        counted = onehot[:, 1, :, :].rearrange("p k n -> p (k n)")[:, 0:2 * (GCOLS // 2)].rearrange("p (s c) -> p s c", s=2)
        rows16 = sb("rows16", [P, 2, UNIT, ROW], BF16)
        w_edge_blk = sb("w_edge_blk", [UNIT * EDIM, UNIT, D])
        w_a = sb("w_a", [P, LAYERS, D + 1])
        w_b = sb("w_b", [P, LAYERS, D + 1])
        w1_a = sb("w1_a", [P, D])
        w2_sb = sb("w2_sb", [D, D])
        bias = sb("bias", [P, LAYERS + 2, D])
        cols = sb("cols", [D, 8])
        bn_st = sb("bn_st", [D, 25, 6])
        bn_mv = sb("bn_mv", [D, 2])
        agg_a = sb("agg_a", [P, WIN])
        agg_b = sb("agg_b", [P, WIN])
        FC = TILES // FOLD
        feat_row = feat[:, :, :].rearrange("p b f -> p (b f)")
        dst_fold_i = [tmp_row[0:FOLD, 0:FC * P].bitcast(I32), tmp_row[0:FOLD, FC * P:2 * FC * P].bitcast(I32)]
        dst_fold = [feat_row[0:FOLD, 0:FC * P], hid_row[0:FOLD, 0:FC * P]]
        ext = sb("ext", [FOLD, 3, FC])
        run = sb("run", [FOLD, 2, FC])
        run_i = sb("run_i", [FOLD, 2, FC], I32)
        e_max = wide[0:WINDOWS, 0:KEYS]
        e_min = wide[0:WINDOWS, KEYS:2 * KEYS]
        G_EXT = GROUPS
        g_ext = spare[0:WINDOWS, G_EXT:G_EXT + 8 * GRANULES].bitcast(F32).rearrange("p (n g) -> p n g", n=4)
        iota_groups = spare[:, 0:GROUPS]
        reach = onehot[:, :, :, :].rearrange("p s k n -> p (s k n)")[:, 0:2 * GROUPS].rearrange("p (s g) -> p s g", s=2)
        scale = sb("scale", [P, 8])
        pow_row = sb("pow_row", [1, P + 4])
        onehot_h = onehot[:, :, :, :].rearrange("p s k n -> p (s k n)").bitcast(F16)
        COUNTED_END = UNIT * WIN + 2 * (GCOLS // 2) + 96
        ident16 = onehot_h[:, COUNTED_END:COUNTED_END + P]
        select = onehot_h[:, COUNTED_END + P:COUNTED_END + P + 2 * GPW]
        CHOSEN = COUNTED_END + P + 2 * GPW
        chosen = onehot_h[:, CHOSEN:CHOSEN + 2 * GPW].rearrange("p (s g) -> p s g", s=2)
        onehot_f = onehot[:, :, :, :].rearrange("p s k n -> p (s k n)").bitcast(F32)
        in_rows = onehot_f[0:PADDED, 0:P]
        iota_i = onehot_f[:, GROUPS:GROUPS + WIN].bitcast(I32)
        ones_f = sb("ones_f", [1, P])
        ones16 = sb("ones16", [P, 1], BF16)
        ones_col = sb("ones_col", [P, 1])
        window_deg = stat[0:GPW, 2:4, :].rearrange("p k n -> p (k n)").rearrange("p (w d) -> p w d", d=GROUP)
        w_d = sb("w_d", [P, LAYERS, D])
        flag = sb("flag", [1, 1], I32)
        norm_l = sb("norm_l", [P, PADDED])
        iota_g = spare[0:WINDOWS, G_EXT + 8 * GRANULES:G_EXT + 10 * GRANULES].bitcast(F32)
        edge_i = sb("edge_i", [WINDOWS, 1], I32)
        lims = sb("lims", [WINDOWS, 6])
        tri = sb("tri", [WINDOWS, WINDOWS + 1])
        bounds = sb("bounds", [1, WINDOWS, 4], I32)
        lo_hot = onehot[:, :, :, 0:P]

        banks = pb("banks", [P, 8, WIN])
        acc_a, acc_b, node_ps, edge0_ps, edge1_ps, small_ps, deg_ps, in_ps = (banks[:, n, :] for n in range(8))
        edge_ps = [edge0_ps, edge1_ps]
        group_ps = [banks[:, 0:2, 0:HALF_BANK], banks[:, 2:4, 0:HALF_BANK]]
        out_ps, inwin_ps = banks[:, 4:6, 0:HALF_BANK], banks[0:GPW, 6:8, 0:HALF_BANK]
        acc_d = [banks[:, 0, :], banks[:, 1, :]]
        agg_d = [agg_a, agg_b]

        s_load = sem("s_load")
        s_w = sem("s_w")
        s_iota = sem("s_iota")
        s_ext = sem("s_ext")
        s_extb = sem("s_extb")
        s_extw = sem("s_extw")
        s_tri = sem("s_tri")
        s_lims = sem("s_lims")
        s_bps = sem("s_bps")
        s_bounds = sem("s_bounds")
        s_hot = [sem(f"s_hot{s}") for s in range(2)]
        s_hist = [sem(f"s_hist{s}") for s in range(2)]
        s_deg = sem("s_deg")
        s_degc = sem("s_degc")
        s_sqrt = sem("s_sqrt")
        s_chain = sem("s_chain")
        s_parts = [sem(f"s_parts{n}") for n in range(LAYERS + 1)]
        s_table = [sem(f"s_table{n}") for n in range(LAYERS + 1)]
        s_x1 = sem("s_x1")
        s_exp_in = sem("s_exp_in")
        s_exp = sem("s_exp")
        s_ln_in = sem("s_ln_in")
        s_ln = sem("s_ln")
        s_bn = sem("s_bn")
        s_bnv = sem("s_bnv")
        s_bns = sem("s_bns")
        s_act = sem("s_act")
        s_mlp = sem("s_mlp")
        s_y = sem("s_y")
        s_final = sem("s_final")
        s_out = sem("s_out")
        s_memset = sem("s_memset")
        s_rows = sem("s_rows")
        s_scan = sem("s_scan")
        s_run = sem("s_run")
        s_runp = sem("s_runp")
        s_reach = [sem(f"s_reach{n}") for n in range(2)]
        s_count = [sem(f"s_count{n}") for n in range(2)]
        s_groups = sem("s_groups")
        s_giota = sem("s_giota")
        s_pair = [sem(f"s_pair{n}") for n in range(2)]
        s_used = [sem(f"s_used{n}") for n in range(2)]
        s_xpair = sem("s_xpair")
        s_xused = sem("s_xused")
        s_degd = [sem(f"s_degd{n}") for n in range(2)]
        s_inwin = sem("s_inwin")
        s_inread = sem("s_inread")
        s_instore = sem("s_instore")
        s_inback = sem("s_inback")
        s_outdeg = sem("s_outdeg")
        s_ident = sem("s_ident")
        s_evac = [sem(f"s_evac{n}") for n in range(2)]
        s_store = [sem(f"s_store{n}") for n in range(2)]
        s_place = [sem(f"s_place{n}") for n in range(2)]
        s_turn_sp = sem("s_turn_sp")
        s_turn_pe = sem("s_turn_pe")
        s_free = [sem(f"s_free{n}") for n in range(2)]
        s_stored = sem("s_stored")
        s_wd = sem("s_wd")
        s_f16 = sem("s_f16")
        s_max = sem("s_max")
        s_maxt = sem("s_maxt")
        s_pow = sem("s_pow")
        s_powb = sem("s_powb")
        s_piece = [sem(f"s_piece{k}") for k in range(PIECES)]
        s_pused = [sem(f"s_pused{k}") for k in range(PIECES)]
        s_dwin = sem("s_dwin")
        s_dagg = sem("s_dagg")
        s_dnode = sem("s_dnode")
        s_dout = sem("s_dout")
        s_flagsum = sem("s_flagsum")
        s_flagin = sem("s_flagin")
        s_flag = sem("s_flag")
        s_gdeg = sem("s_gdeg")
        s_gsqrt = sem("s_gsqrt")
        s_dexp_in = sem("s_dexp_in")
        s_dexp = sem("s_dexp")

        class EdgeSems:
            def __init__(self, n):
                self.idx = [sem(f"s_idx{n}_{s}") for s in range(2)]
                self.rows = [[sem(f"s_rows{n}_{s}_{i}") for s in range(2)] for i in range(LAYERS if n == 0 else 1)]
                self.read = n < LAYERS and [sem(f"s_read{n}_{s}") for s in range(2)]
                self.attr = n == LAYERS and [sem(f"s_attr{n}_{s}") for s in range(2)]
                self.hot = [sem(f"s_onehot{n}_{s}") for s in range(2)]
                self.sum = [sem(f"s_sum{n}_{s}") for s in range(2)]
                self.ea = n == LAYERS and [sem(f"s_ea{n}_{s}") for s in range(2)]
                self.msg = n == LAYERS and [sem(f"s_msg{n}_{s}") for s in range(2)]
                self.p1 = n == LAYERS and [sem(f"s_p1{n}_{s}") for s in range(2)]
                self.r1 = n == LAYERS and [sem(f"s_r1{n}_{s}") for s in range(2)]
                self.p2 = n == LAYERS and [sem(f"s_p2{n}_{s}") for s in range(2)]
                self.p3 = n == LAYERS and [sem(f"s_p3{n}_{s}") for s in range(2)]
                self.issue = sem(f"s_issue{n}")
                self.win = sem(f"s_win{n}")
                self.agg = sem(f"s_agg{n}")
                self.node = sem(f"s_node{n}")
                self.nodec = sem(f"s_nodec{n}")
                self.fwin = n == LAYERS and sem(f"s_fwin{n}")

        GIN = LAYERS
        gathered_sems, gin_sems = EdgeSems(0), EdgeSems(GIN)
        es = [gathered_sems] * LAYERS + [gin_sems]
        block = ctx.enter_context(nc.Block())

        def limits(engine, w):
            first = engine.value_load(bounds[0:1, bass.ds(w, 1), 0], min_val=0, max_val=WINDOWS * GRANULES)
            end = engine.value_load(bounds[0:1, bass.ds(w, 1), 1], min_val=1, max_val=WINDOWS * GRANULES)
            return first, end

        def steps_ahead(engine, w):
            return engine.value_load(bounds[0:1, bass.ds(w, 1), 2], min_val=0, max_val=WINDOWS * GRANULES)

        def steps_before(engine, n):
            if n in (0, GIN):
                return 0
            return engine.value_load(bounds[0:1, WINDOWS - 1, 1:2], min_val=1, max_val=WINDOWS * GRANULES) * n

        def windows_before(n):
            return 0 if n == GIN else n * WINDOWS

        def granule(engine, j, ahead):
            return nc.s_assert_within(engine.snap(j - ahead), 0, GRANULES - 1, skip_runtime_bounds_check_because="bounds are clamped")


        def pair_word(engine, q):
            word = engine.value_load(group_word[0:1, bass.ds(q, 1)], min_val=0, max_val=4 * SHIFT * SHIFT - 1)
            tiles = [nc.s_assert_within(engine.snap(t), 0, TILES - DENSE, skip_runtime_bounds_check_because="bounds are clamped")
                     for t in (word % SHIFT, word // SHIFT % SHIFT)]
            flags = engine.snap(word // (SHIFT * SHIFT))
            return tiles, [engine.snap(flags % 2), engine.snap(flags // 2)], flags

        def beyond(engine, g, more, tile):
            with engine.If(more > 0):
                first = engine.value_load(group_p[0:1, bass.ds(g, 1)], min_val=0, max_val=GROUPS * TILES)
                end = engine.value_load(group_p[0:1, bass.ds(g + 1, 1)], min_val=1, max_val=GROUPS * TILES)
                ahead = engine.value_load(group_d[0:1, bass.ds(g, 1)], min_val=0, max_val=(GROUPS + 1) * TILES)
                with engine.Fori(first, end) as i:
                    t = engine.snap(i + (TILES + DENSE) - ahead)
                    tile(i, nc.s_assert_within(t, 0, TILES - 1, skip_runtime_bounds_check_because="bounds are clamped"))

        def other_slot(i):
            return i % OTHERS + 2 * DENSE

        def at(ring, slot):
            return ring[:, bass.ds(slot, 1), :].rearrange("p r c -> p (r c)")

        @block.sync
        def _(sp):
            for h in range(2):
                sp.sem_inc(s_free[h], 1)
            sp.dma_start(src_key[:, 0:TILES], src).then_inc(s_load, 16)
            sp.dma_start(keys_i[:, 0:TILES], dst).then_inc(s_load, 16)
            sp.dma_start(dst_fold_i[0], dst_tiles).then_inc(s_load, 16)
            sp.dma_start(dst_fold_i[1], dst_back).then_inc(s_load, 16)
            sp.wait_ge(s_memset, 1)
            for n in range(LAYERS):
                for part in range(2):
                    sp.dma_start(w_a[part * D:(part + 1) * D, n, 0:D], w_l0[n]).then_inc(s_w, 16)
                    sp.dma_start(w_d[part * D:(part + 1) * D, n, :], w_l0[n]).then_inc(s_w, 16)
                sp.dma_start(w_b[0:D, n, 0:D], w_l0[n]).then_inc(s_w, 16)
                sp.dma_start(bias[:, n, :], b_l0[n].to_broadcast([P, D])).then_inc(s_w, 16)
            for part in range(2):
                sp.dma_start(w1_a[part * D:(part + 1) * D, :], w1).then_inc(s_w, 16)
            for k in range(UNIT):
                sp.dma_start(w_edge_blk[k * EDIM:(k + 1) * EDIM, k, :], w_edge).then_inc(s_w, 16)
            sp.dma_start(w2_sb[:, :], w2).then_inc(s_w, 16)
            sp.dma_start(bias[:, LAYERS, :], b_edge.to_broadcast([P, D])).then_inc(s_w, 16)
            sp.dma_start(bias[:, LAYERS + 1, :], b2.to_broadcast([P, D])).then_inc(s_w, 16)
            for n, v in enumerate((b1, gamma, beta)):
                sp.dma_start(cols[:, n:n + 1], v).then_inc(s_w, 16)
            sp.wait_ge(s_ext, 1)
            for n in range(2):
                sp.dma_start(extremes[n:n + 1, :].rearrange("o (p t) -> p (o t)", p=FOLD), ext[:, n, :]).then_inc(s_extb, 16)
            sp.dma_start(running[1:2, :].rearrange("o (p t) -> p (o t)", p=FOLD), ext[:, 2, :]).then_inc(s_extb, 16)
            sp.wait_ge(s_extb, 48)
            sp.dma_start(row_buf[:, 0, :], extremes[0:1, :]).then_inc(s_rows, 16)
            sp.dma_start(row_buf[:, 1, :], running[1:2, :]).then_inc(s_rows, 16)
            sp.wait_ge(s_scan, 1)
            sp.dma_start(e_max[:, 0:TILES], extremes[0:1, :].to_broadcast([WINDOWS, TILES])).then_inc(s_extw, 16)
            sp.dma_start(e_min[:, 0:TILES], extremes[1:2, :].to_broadcast([WINDOWS, TILES])).then_inc(s_extw, 16)
            sp.wait_ge(s_rows, 32)
            for n in range(2):
                sp.dma_start(running[n:n + 1, :], row_buf[:, n, :]).then_inc(s_run, 16)
            sp.wait_ge(s_run, 32)
            for n in range(2):
                sp.dma_start(run[:, n, :], running[n:n + 1, :].rearrange("o (p t) -> p (o t)", p=FOLD)).then_inc(s_runp, 16)
            sp.wait_ge(s_groups, 1)
            sp.dma_start(feat[:, 0:FULL_BLOCKS, :], x[0:FULL_BLOCKS * P, :].rearrange("(b p) f -> p b f", p=P)).then_inc(s_x1, 16)
            sp.dma_start(feat[0:REST, FULL_BLOCKS, :], x[FULL_BLOCKS * P:NODES, :]).then_inc(s_x1, 16)
            with sp.Fori(0, WINDOWS) as w:
                for h in range(2):
                    for s in range(2):
                        sp.wait_ge(s_place[s], (w * 2 + h + 1) * (GPH // 2) + 1)
                    sp.sem_inc(s_turn_sp, 1)
                    sp.dma_start(counts[bass.ds(w, 1), h, :, :].rearrange("w p n -> (w p) n"), win_words[h]).then_inc(s_store[h], 16)
                    sp.wait_ge(s_store[h], (w + 1) * 16)
                    sp.sem_inc(s_free[h], 1)
            sp.sem_inc(s_stored, 1)
            sp.wait_ge(s_inread, WINDOWS + 1)
            sp.dma_start(degrees.rearrange("w g d -> g w d"), window_deg[:, :, :]).then_inc(s_instore, 16)
            sp.wait_ge(s_instore, 16)
            sp.dma_start(in_rows, degrees.rearrange("w (b g) d -> (w b) (g d)", b=WB)).then_inc(s_inback, 16)
            for n in range(LAYERS):
                with sp.Fori(0, WINDOWS) as w:
                    for k in range(PIECES):
                        sp.wait_ge(s_pused[k], w + (n * WINDOWS + 1))
                        sp.sem_inc(s_turn_sp, 1)
                        sp.dma_start(piece_words[:, k, :, :], counts[bass.ds(w, 1), :, :, k * PB * HALF // 4:(k + 1) * PB * HALF // 4]
                                     .rearrange("w h p n -> p (w h) n")).then_inc(s_piece[k], 16)
            sp.wait_ge(s_bounds, 1)

            def edge_tables(n):
                sp.wait_ge(s_parts[n], 1)
                if n < LAYERS:
                    sp.dma_start(table16.rearrange("(b p) f -> p b f", p=P), parts[:, :, :]).then_inc(s_table[n], 16)
                else:
                    sp.dma_start(table32.rearrange("(b p) f -> p b f", p=P), tmp[:, 0:BLOCKS, :]).then_inc(s_table[n], 16)
                e = es[n]
                before = steps_before(sp, n)
                with sp.Fori(0, WINDOWS) as w:
                    first, end = limits(sp, w)
                    ahead = steps_ahead(sp, w)
                    with sp.Fori(first, end) as j:
                        g = granule(sp, j, ahead)
                        c = j + before
                        for s in range(2):
                            sp.wait_ge(e.msg[s] if n == GIN else e.read[s], c + 1)
                            sp.dma_start(idx[:, s, :], src_key[:, bass.ds(g * GRAN + s * UNIT, UNIT)]).then_inc(e.idx[s], 16)
                            if n == GIN:
                                sp.wait_ge(e.ea[s], c + 1)
                                u = g * 2 + s
                                if s == 1:
                                    u = u - u // UNITS
                                u = nc.s_assert_within(u, 0, UNITS - 1, skip_runtime_bounds_check_because="bounds are clamped")
                                sp.dma_start(attr_sb[:, s, :], attr[bass.ds(u, 1), :, :].rearrange("u k p -> (u k) p")).then_inc(e.attr[s], 16)
            sp.wait_ge(s_flag, 1)
            flagged = sp.value_load(flag[0:1, 0:1], min_val=0, max_val=1)
            with sp.If(flagged > 0):
                for n in range(LAYERS):
                    edge_tables(n)
            edge_tables(GIN)
            steps = sp.value_load(bounds[0:1, WINDOWS - 1, 1:2], min_val=1, max_val=WINDOWS * GRANULES)
            for s in range(2):
                sp.wait_ge(es[GIN].ea[s], steps + 1)
                sp.sem_inc(s_turn_sp, 1)
                sp.dma_start(attr_sb[:, s, :], attr[s, :, :]).then_inc(es[GIN].attr[s], 16)
            sp.wait_ge(s_final, 1)
            sp.dma_start(out[0:FULL_BLOCKS * P, :].rearrange("(b p) f -> p b f", p=P), feat[:, 0:FULL_BLOCKS, :]).then_inc(s_out, 16)
            sp.dma_start(out[FULL_BLOCKS * P:NODES, :], feat[0:REST, FULL_BLOCKS, :]).then_inc(s_out, 16)
            sp.wait_ge(s_out, 32)

        @block.gpsimd
        def _(pool):
            nc.gpsimd.iota(iota_i[:, :], [[1, WIN]], base=0, channel_multiplier=0).then_inc(s_iota, 1)
            nc.gpsimd.iota(edge_i[:, :], [[0, 1]], base=0, channel_multiplier=WIN).then_inc(s_iota, 1)
            nc.gpsimd.memset(ident[:, :], 0.0).then_inc(s_tri, 1)
            nc.gpsimd.memset(tri[:, :], 1.0).then_inc(s_tri, 1)
            pool.wait_ge(s_tri, 2)
            nc.gpsimd.affine_select(out=ident[:, :], in_=ident[:, :], pattern=[[-1, P]], compare_op=ALU.not_equal,
                                    fill=1.0, base=0, channel_multiplier=1).then_inc(s_tri, 1)
            nc.gpsimd.affine_select(out=tri[:, :], in_=tri[:, :], pattern=[[1, WINDOWS + 1]], compare_op=ALU.is_gt,
                                    fill=0.0, base=0, channel_multiplier=-1).then_inc(s_tri, 1)
            nc.gpsimd.iota(iota_groups[:, :], [[1, GROUPS]], base=0, channel_multiplier=0,
                           allow_small_or_imprecise_dtypes=True).then_inc(s_giota, 1)
            nc.gpsimd.iota(iota_key, [[1, BLOCKS], [BLOCKS, GROUP]], base=0, channel_multiplier=0,
                           allow_small_or_imprecise_dtypes=True).then_inc(s_giota, 1)
            nc.gpsimd.iota(group_base, [[GCOLS, GROUPS]], base=0, channel_multiplier=0,
                           allow_small_or_imprecise_dtypes=True).then_inc(s_giota, 1)
            pool.wait_ge(s_bounds, 1)
            def gather(n):
                e = es[n]
                rows_ready = e.rows[n % LAYERS]
                before = steps_before(pool, n)
                pool.wait_ge(s_table[n], 16)
                steps = pool.value_load(bounds[0:1, WINDOWS - 1, 1:2], min_val=1, max_val=WINDOWS * GRANULES)
                with pool.Fori(0, steps) as j:
                    c = j + before
                    for s in range(2):
                        pool.wait_ge(e.idx[s], (c + 1) * 16)
                        pool.wait_ge(e.msg[s] if n == GIN else e.sum[s], c + 1)
                        pool.sem_inc(e.issue, 1)
                        for k in range(UNIT):
                            nc.gpsimd.indirect_dma_start(
                                out=rows32[:, s, k, :] if n == GIN else rows16[:, s, k, 0:HIDDEN], out_offset=None,
                                in_=(table32 if n == GIN else table16)[:, :],
                                in_offset=bass.IndirectOffsetOnAxis(ap=idx[:, s, k:k + 1], axis=0),
                            ).then_inc(rows_ready[s], 16)

            pool.wait_ge(s_flag, 1)
            flagged = pool.value_load(flag[0:1, 0:1], min_val=0, max_val=1)
            with pool.If(flagged > 0):
                for n in range(LAYERS):
                    gather(n)
            gather(GIN)

        @block.vector
        def _(dve):
            for c in (es[GIN].msg[0], es[GIN].msg[1], es[GIN].p3[0], es[GIN].p3[1], s_y, s_inread):
                dve.sem_inc(c, 1)
            count = [0]

            def link(ins):
                count[0] += 1
                ins.then_inc(s_chain, 1)
                dve.wait_ge(s_chain, count[0])

            V = nc.vector
            V.memset(w_a[:, :, :], 0.0)
            V.memset(w_edge_blk[:, :, :], 0.0)
            V.memset(bounds[:, :, :], 0)
            V.memset(src_key[:, TILES:], 0)
            V.memset(zeros16[:, :], 0.0)
            V.memset(feat[:, FULL_BLOCKS:, :], 0.0)
            V.memset(rows16[:, :, :, HIDDEN + 1:], 0.0)
            V.memset(rows16[:, :, :, HIDDEN:HIDDEN + 1], 1.0)
            link(V.memset(w_b[:, :, :], 0.0))
            V.memset(w_b[D:D + 1, :, D:D + 1], 1.0).then_inc(s_memset, 1)
            dve.wait_ge(s_memset, 1)
            dve.wait_ge(s_iota, 2)
            V.tensor_copy(iota_g[:, :], iota_i[0:WINDOWS, 0:GRANULES])
            V.tensor_copy(lims[:, 0:1], edge_i[:, :])
            link(V.tensor_copy(iota_win[:, :], iota_i[:, :]))
            link(V.tensor_scalar(win_base[:, :], iota_win[:, 0:WINDOWS], float(WIN), None, ALU.mult))
            link(V.tensor_scalar(lims[:, 1:2], lims[:, 0:1], float(WIN), None, ALU.add))
            V.memset(ones_f[:, :], 1.0)
            V.memset(ones16[:, :], 1.0)
            V.memset(ones_col[:, :], 1.0)
            dve.wait_ge(s_tri, 4)
            V.tensor_copy(ident16[:, :], ident[:, :])
            link(V.memset(select[:, :], 0.0))
            V.memset(select[:, GPW - 1:GPW], 1.0).then_inc(s_ident, 1)
            dve.wait_ge(s_load, 64)
            V.memset(dst_key[:, TILES:], -1.0)
            V.tensor_copy(dst_key[:, 0:TILES], keys_i[:, 0:TILES])
            V.tensor_copy(dst_fold[0], dst_fold_i[0])
            link(V.tensor_copy(dst_fold[1], dst_fold_i[1]))
            fold3 = [f.rearrange("p (t e) -> p t e", e=P) for f in dst_fold]
            V.tensor_reduce(ext[:, 0, :], fold3[0], axis=AX.X, op=ALU.max)
            V.tensor_reduce(ext[:, 1, :], fold3[0], axis=AX.X, op=ALU.min)
            last = V.tensor_reduce(ext[:, 2, :], fold3[1], axis=AX.X, op=ALU.min)
            last.then_inc(s_ext, 1)
            dve.wait_ge(s_ext, 1)
            def src_digits():
                link(V.tensor_scalar(digit_i, src_key[:, :], P - 1, None, ALU.bitwise_and))
                V.tensor_copy(src_lo, digit_i)
                link(V.tensor_scalar(keys_i, src_key[:, :], P.bit_length() - 1, None, ALU.logical_shift_right))
                link(V.tensor_copy(src_hi, keys_i))

            src_digits()
            link(V.scalar_tensor_tensor(out=pair_key, in0=dst_key[:, :], scalar=float(BLOCKS), in1=src_hi, op0=ALU.mult, op1=ALU.add))
            dve.wait_ge(s_rows, 32)
            V.tensor_tensor_scan(row_buf[:, 0, :], row_buf[:, 0, :], row_buf[:, 0, :], -1.0, ALU.max, ALU.max)
            V.tensor_tensor_scan(row_buf[:, 1, :], row_buf[:, 1, :], row_buf[:, 1, :], BIG, ALU.min, ALU.min).then_inc(s_scan, 1)
            dve.wait_ge(s_runp, 32)
            link(V.tensor_copy(run_i[:, :, :], run[:, :, :]))
            link(V.tensor_scalar(run_i[:, :, :], run_i[:, :, :], GROUP.bit_length() - 1, None, ALU.logical_shift_right))
            link(V.tensor_copy(run[:, :, :], run_i[:, :, :]))
            dve.wait_ge(s_giota, 3)
            for c in range(FC):
                for n in range(2):
                    if c:
                        dve.wait_ge(s_count[n], c)
                    V.tensor_scalar(reach[0:FOLD, n, :], iota_groups[0:FOLD, :], run[:, n, c:c + 1], None,
                                    ALU.is_ge if n else ALU.is_gt).then_inc(s_reach[n], 1)
            for n in range(2):
                dve.wait_ge(s_count[n], FC)
                link(V.tensor_copy(count_row[:, n, :].rearrange("p (a g) -> p a g", a=4), banks[0:1, 4 * n:4 * n + 4, 0:GROUPS // 4]))
            g_lo, g_hi, g_n, g_p = (count_row[:, n, :] for n in range(4))
            link(V.tensor_scalar(g_lo, g_lo, float(TILES - DENSE), None, ALU.min))
            link(V.tensor_tensor(g_n, g_hi, g_lo, ALU.subtract))
            link(V.tensor_scalar(g_n, g_n, float(DENSE), 0.0, ALU.subtract, ALU.max))
            V.memset(group_p[:, 0:1], 0)
            link(V.tensor_tensor_scan(g_p, g_n, g_n, 0.0, ALU.add, ALU.bypass))
            V.tensor_copy(group_p[:, 1:GROUPS + 1], g_p)
            link(V.tensor_tensor(g_p, g_p, g_n, ALU.subtract))
            link(V.tensor_tensor(g_p, g_p, g_lo, ALU.subtract))
            link(V.tensor_scalar(g_p, g_p, float(TILES), None, ALU.add))
            V.tensor_copy(group_d, g_p)
            link(V.tensor_scalar(g_n, g_n, 1.0, None, ALU.min))
            lo2, n2 = (v.rearrange("p (q s) -> p q s", s=2) for v in (g_lo, g_n))
            link(V.scalar_tensor_tensor(out=n2[:, :, 0], in0=n2[:, :, 1], scalar=2.0, in1=n2[:, :, 0], op0=ALU.mult, op1=ALU.add))
            link(V.scalar_tensor_tensor(out=lo2[:, :, 0], in0=lo2[:, :, 1], scalar=float(SHIFT), in1=lo2[:, :, 0], op0=ALU.mult, op1=ALU.add))
            V.tensor_copy(group_word, lo2[:, :, 0])
            link(V.tensor_copy(group_flags, n2[:, :, 0]))
            link(V.tensor_scalar(group_flags, group_flags, 2 * (SHIFT.bit_length() - 1), None, ALU.logical_shift_left))
            V.tensor_tensor(group_word, group_word, group_flags, ALU.bitwise_or).then_inc(s_groups, 1)
            V.memset(e_max[:, TILES:], -1.0)
            link(V.memset(e_min[:, TILES:], BIG))
            dve.wait_ge(s_extw, 32)
            V.tensor_reduce(g_ext[:, 0, :], e_max.rearrange("p (g t) -> p g t", t=GRAN), axis=AX.X, op=ALU.max)
            link(V.tensor_reduce(g_ext[:, 1, :], e_min.rearrange("p (g t) -> p g t", t=GRAN), axis=AX.X, op=ALU.min))
            link(V.tensor_scalar(g_ext[:, 2, :], g_ext[:, 0, :], lims[:, 0:1], BIG, ALU.is_lt, ALU.mult))
            link(V.tensor_tensor(g_ext[:, 0, :], g_ext[:, 2, :], iota_g[:, :], ALU.add))
            link(V.tensor_reduce(lims[:, 2:3], g_ext[:, 0, :], axis=AX.X, op=ALU.min))
            link(V.tensor_scalar(g_ext[:, 2, :], g_ext[:, 1, :], lims[:, 1:2], None, ALU.is_lt))
            link(V.tensor_scalar(g_ext[:, 3, :], iota_g[:, :], 1.0, None, ALU.add))
            link(V.tensor_tensor(g_ext[:, 1, :], g_ext[:, 2, :], g_ext[:, 3, :], ALU.mult))
            link(V.tensor_reduce(lims[:, 3:4], g_ext[:, 1, :], axis=AX.X, op=ALU.max))
            link(V.tensor_scalar(lims[:, 2:3], lims[:, 2:3], float(GRANULES - 1), None, ALU.min))
            link(V.tensor_tensor(lims[:, 4:5], lims[:, 3:4], lims[:, 2:3], ALU.subtract))
            link(V.tensor_scalar(lims[:, 4:5], lims[:, 4:5], 1.0, None, ALU.max))
            V.tensor_scalar(lims[:, 5:6], lims[:, 2:3], -1.0, None, ALU.mult).then_inc(s_lims, 1)
            dve.wait_ge(s_bps, 1)
            V.tensor_copy(bounds[:, :, 0], small_ps[0:1, 0:WINDOWS])
            V.tensor_copy(bounds[:, :, 1], small_ps[0:1, 1:WINDOWS + 1])
            V.tensor_copy(bounds[:, :, 2], small_ps[0:1, 32:32 + WINDOWS]).then_inc(s_bounds, 1)
            with V.Fori(0, WINDOWS) as w:
                with V.Fori(0, GPW // 2) as m:
                    q = w * (GPW // 2) + m
                    tiles, more, either = pair_word(V, q)
                    def tile(g, t, slot):
                        V.tensor_scalar(at(lo_ring, slot), iota_win[:, 0:P], src_lo[:, bass.ds(t, 1)], None, ALU.is_equal)
                        return V.tensor_scalar(at(key_hot, slot), iota_key, group_base[:, bass.ds(g, 1)],
                                               pair_key[:, bass.ds(t, 1)], ALU.add, ALU.is_equal)

                    for s in range(2):
                        for k in range(DENSE):
                            dve.wait_ge(s_used[s], q * DENSE + (k + 1))
                            tile(q * 2 + s, tiles[s] + k, s * DENSE + k).then_inc(s_pair[s], 1)
                    with V.If(either > 0):
                        for s in range(2):
                            def other(i, t):
                                dve.wait_ge(s_xused, i + 1)
                                tile(q * 2 + s, t, other_slot(i)).then_inc(s_xpair, 1)

                            beyond(V, q * 2 + s, more[s], other)
                dve.wait_ge(s_inwin, w + 1)
                V.tensor_reduce(window_deg[:, bass.ds(w, 1), :].rearrange("p w d -> p (w d)"), inwin_ps.rearrange("p a (b d) -> p d a b", d=GROUP), axis=AX.XY,
                                op=ALU.add).then_inc(s_inread, 1)
            dve.wait_ge(s_outdeg, 1)
            for a in range(2):
                last = V.tensor_reduce(stat[:, 0, a * (BLOCKS // 2):(a + 1) * (BLOCKS // 2)], out_ps[:, a, :].rearrange("p (b d) -> p b d", d=GROUP), axis=AX.X, op=ALU.add)
            link(last)
            V.tensor_reduce(scale[:, 5:6], stat[:, 0, 0:BLOCKS], axis=AX.X, op=ALU.add).then_inc(s_flagin, 1)
            dve.wait_ge(s_flagin, 1)
            V.tensor_scalar(stat[:, 0, 0:BLOCKS], stat[:, 0, 0:BLOCKS], 1.0 / UNIT_COUNT, 1.0, ALU.mult, ALU.max).then_inc(s_degc, 1)
            dve.wait_ge(s_sqrt, 1)
            link(V.reciprocal(out_norm[:, 0:BLOCKS], stat[:, 1, 0:BLOCKS]))
            dve.wait_ge(s_x1, 32)
            dve.wait_ge(s_stored, 1)

            def over(vec):
                return vec[:, 0:BLOCKS].rearrange("p (b o) -> p b o", o=1).to_broadcast([P, BLOCKS, D])

            def row(n):
                return bias[:, n:n + 1, :].to_broadcast([P, BLOCKS, D])

            T, H, X = tmp[:, 0:BLOCKS, :], hid[:, 0:BLOCKS, 0:D], feat[:, 0:BLOCKS, :]

            def split(n):
                link(V.tensor_copy(parts[:, :, 0:D], T))
                link(V.tensor_tensor(T, T, parts[:, :, 0:D], ALU.subtract))
                link(V.tensor_copy(parts[:, :, D:2 * D], T))
                V.tensor_tensor(parts[:, :, 2 * D:3 * D], T, parts[:, :, D:2 * D], ALU.subtract).then_inc(s_parts[n], 1)

            def layer_norm(n):
                link(V.tensor_reduce(stat[:, 0, 0:BLOCKS], X, axis=AX.X, op=ALU.add))
                link(V.tensor_scalar(stat[:, 0, 0:BLOCKS], stat[:, 0, 0:BLOCKS], 1.0 / D, None, ALU.mult))
                link(V.tensor_tensor(X, X, over(stat[:, 0, :]), ALU.subtract))
                link(V.tensor_tensor(T, X, X, ALU.mult))
                link(V.tensor_reduce(stat[:, 1, 0:BLOCKS], T, axis=AX.X, op=ALU.add))
                V.tensor_scalar(stat[:, 2, 0:BLOCKS], stat[:, 1, 0:BLOCKS], 1.0 / D, LN_EPS, ALU.mult, ALU.add).then_inc(s_ln_in, 1)
                dve.wait_ge(s_ln, n + 1)
                link(V.reciprocal(stat[:, 3, 0:BLOCKS], stat[:, 0, 0:BLOCKS]))

            def split16(n):
                link(V.tensor_reduce(scale[:, 2:3], T, axis=AX.XY, op=ALU.max))
                link(V.tensor_reduce(scale[:, 3:4], T, axis=AX.XY, op=ALU.min))
                link(V.tensor_scalar(scale[:, 3:4], scale[:, 3:4], -1.0, None, ALU.mult))
                V.tensor_tensor(scale[:, 4:5], scale[:, 2:3], scale[:, 3:4], ALU.max).then_inc(s_max, 1)
                dve.wait_ge(s_maxt, n + 1)
                link(V.tensor_reduce(pow_row[:, 0:1], small_ps[0:1, 0:P], axis=AX.X, op=ALU.max))
                link(V.tensor_scalar(pow_row[:, 0:1], pow_row[:, 0:1], 2.0 ** -100, None, ALU.max))
                link(V.tensor_scalar(pow_row[:, 1:2].bitcast(I32), pow_row[:, 0:1].bitcast(I32), 0x7F800000, None, ALU.bitwise_and))
                V.reciprocal(pow_row[:, 2:3], pow_row[:, 1:2]).then_inc(s_pow, 1)
                dve.wait_ge(s_powb, n + 1)
                link(V.tensor_copy(scale[:, 0:2], small_ps[:, 256:258]))
                link(V.tensor_scalar(T, T, scale[:, 1:2], None, ALU.mult))
                link(V.tensor_copy(rows_f16[:, :, 0:D], T))
                link(V.tensor_tensor(T, T, rows_f16[:, :, 0:D], ALU.subtract))
                V.tensor_scalar(rows_f16[:, :, D:2 * D], T, LO_SCALE, None, ALU.mult).then_inc(s_f16, 1)

            dve.wait_ge(s_w, 16 * (6 * LAYERS + 2 + UNIT + 6))
            V.tensor_scalar(w_d[D:2 * D, :, :], w_d[D:2 * D, :, :], 1.0 / LO_SCALE, None, ALU.mult).then_inc(s_wd, 1)
            link(V.tensor_tensor(T, X, over(out_norm), ALU.mult))
            for n in range(LAYERS):
                split16(n)
                dve.wait_ge(s_dout, (n + 1) * WINDOWS + 1)
                if n == 0:
                    dve.wait_ge(s_flagsum, 1)
                    V.tensor_scalar(stat[:, 0, 0:BLOCKS], small_ps[:, 384:384 + BLOCKS], 1.0 / UNIT_COUNT, 1.0, ALU.mult, ALU.max).then_inc(s_degc, 1)
                    V.tensor_scalar(flag[:, :], small_ps[0:1, 300:301], UNIT_COUNT * EDGES, None, ALU.not_equal).then_inc(s_flag, 1)
                    dve.wait_ge(s_sqrt, 2)
                    link(V.reciprocal(in_norm[:, 0:BLOCKS], stat[:, 1, 0:BLOCKS]))
                link(V.tensor_scalar(norm_l[:, 0:BLOCKS], in_norm[:, 0:BLOCKS], scale[:, 0:1], 1.0 / UNIT_COUNT, ALU.mult, ALU.mult))
                link(V.tensor_tensor(H, H, over(norm_l), ALU.mult))
                link(V.tensor_tensor(H, H, row(n), ALU.add))
                V.tensor_scalar(T, H, 0.0, None, ALU.min).then_inc(s_dexp_in, 1)
                dve.wait_ge(s_dexp, n + 1)
                link(V.tensor_scalar(H, H, 0.0, None, ALU.max))
                link(V.scalar_tensor_tensor(out=T, in0=T, scalar=-1.0, in1=H, op0=ALU.add, op1=ALU.add))
                if n < LAYERS - 1:
                    link(V.tensor_tensor(T, T, over(out_norm), ALU.mult))

            def edge_sums(n):
                e = es[n]
                before = steps_before(V, n)
                with V.Fori(0, WINDOWS) as w:
                    first, end = limits(V, w)
                    ahead = steps_ahead(V, w)
                    with V.Fori(first, end) as j:
                        g = granule(V, j, ahead)
                        c = j + before
                        for s in range(2):
                            def hot(k):
                                return V.tensor_scalar(onehot[:, s, k, :], iota_win[:, :], win_base[:, bass.ds(w, 1)],
                                                       dst_key[:, bass.ds(g * GRAN + s * UNIT + k, 1)], ALU.add, ALU.is_equal)
                            if n == GIN:
                                dve.wait_ge(e.rows[0][s], (c + 1) * (16 * UNIT))
                                dve.wait_ge(e.ea[s], c + 2)
                                dve.wait_ge(e.p3[s], c + 1)
                                V.tensor_tensor(msg[:, s, :, :], edge_ps[s][:, 0:UNIT * D].rearrange("p (k f) -> p k f", f=D),
                                                rows32[:, s, :, :], ALU.add).then_inc(e.msg[s], 1)
                            dve.wait_ge(e.sum[s], c + 1)
                            for k in range(UNIT):
                                last = hot(k)
                            last.then_inc(e.hot[s], 1)
                            if n == GIN:
                                dve.wait_ge(e.p1[s], c + 1)
                                V.scalar_tensor_tensor(out=left[:, s, :, :], in0=msg[:, s, :, :], scalar=0.0, in1=rows16[:, s, :, 0:D],
                                                       op0=ALU.max, op1=ALU.subtract).then_inc(e.r1[s], 1)
                                dve.wait_ge(e.p2[s], c + 1)
                                V.tensor_tensor(rows16[:, s, :, 2 * D:3 * D], left[:, s, :, :], rows16[:, s, :, D:2 * D],
                                                ALU.subtract).then_inc(e.p3[s], 1)

            def gathered_layer(n):
                if n == 0:
                    src_digits()
                    link(V.memset(src_hi[:, TILES:], -1.0))
                    with V.Fori(0, GRANULES) as g:
                        for s in range(2):
                            dve.wait_ge(s_hist[s], g + 1)
                            for k in range(UNIT):
                                t = g * GRAN + s * UNIT + k
                                V.tensor_scalar(lo_hot[:, s, k, :], iota_win[:, 0:P], src_lo[:, bass.ds(t, 1)], None, ALU.is_equal)
                                last = V.tensor_scalar(hi_hot[:, s, k, :], iota_win[:, 0:BLOCKS], src_hi[:, bass.ds(t, 1)], None, ALU.is_equal)
                            last.then_inc(s_hot[s], 1)
                    dve.wait_ge(s_deg, 1)
                    V.tensor_scalar(stat[:, 0, 0:BLOCKS], deg_ps[:, 0:BLOCKS], 1.0, None, ALU.max).then_inc(s_gdeg, 1)
                    dve.wait_ge(s_gsqrt, 1)
                    link(V.reciprocal(out_norm[:, 0:BLOCKS], stat[:, 1, 0:BLOCKS]))
                    link(V.tensor_tensor(T, X, over(out_norm), ALU.mult))
                    split(0)
                edge_sums(n)
                e = es[n]
                dve.wait_ge(e.nodec, (n + 1) * WINDOWS + 1)
                if n == 0:
                    V.tensor_scalar(stat[:, 0, 0:BLOCKS], hid[:, 0:BLOCKS, D], 1.0, None, ALU.max).then_inc(s_gdeg, 1)
                    dve.wait_ge(s_gsqrt, 2)
                    link(V.reciprocal(in_norm[:, 0:BLOCKS], stat[:, 1, 0:BLOCKS]))
                link(V.tensor_tensor(H, H, over(in_norm), ALU.mult))
                link(V.tensor_tensor(H, H, row(n), ALU.add))
                V.tensor_scalar(T, H, 0.0, None, ALU.min).then_inc(s_exp_in, 1)
                dve.wait_ge(s_exp, n + 1)
                link(V.tensor_scalar(H, H, 0.0, None, ALU.max))
                if n < LAYERS - 1:
                    link(V.scalar_tensor_tensor(out=T, in0=T, scalar=-1.0, in1=H, op0=ALU.add, op1=ALU.add))
                    link(V.tensor_tensor(T, T, over(out_norm), ALU.mult))
                    dve.wait_ge(s_table[n], 16)
                    split(n + 1)
                else:
                    link(V.scalar_tensor_tensor(out=T, in0=T, scalar=-1.0, in1=H, op0=ALU.add, op1=ALU.add))

            flagged = V.value_load(flag[0:1, 0:1], min_val=0, max_val=1)
            before = count[0]
            with V.If(flagged > 0):
                for n in range(LAYERS):
                    gathered_layer(n)
            with V.Else():
                dve.sem_inc(s_chain, count[0] - before)
            link(V.tensor_tensor(X, X, T, ALU.add))
            layer_norm(0)
            link(V.tensor_tensor(X, X, over(stat[:, 3, :]), ALU.mult))
            V.tensor_tensor(T, X, row(LAYERS), ALU.add).then_inc(s_parts[GIN], 1)
            edge_sums(GIN)
            dve.wait_ge(es[GIN].nodec, WINDOWS + 1)
            for c in range(NODES // 500):
                last = V.bn_stats(bn_st[:, c, :], hiddenT[:, c * 500:(c + 1) * 500])
            link(last)
            link(V.bn_aggr(bn_mv[:, :], bn_st[:, :, :].rearrange("p c s -> p (c s)")))
            V.tensor_scalar(cols[:, 3:4], bn_mv[:, 1:2], BN_EPS, None, ALU.add).then_inc(s_bnv, 1)
            dve.wait_ge(s_bns, 1)
            link(V.reciprocal(cols[:, 5:6], cols[:, 4:5]))
            link(V.tensor_tensor(cols[:, 6:7], cols[:, 5:6], cols[:, 1:2], ALU.mult))
            link(V.tensor_tensor(cols[:, 5:6], cols[:, 6:7], bn_mv[:, 0:1], ALU.mult))
            V.tensor_tensor(cols[:, 7:8], cols[:, 2:3], cols[:, 5:6], ALU.subtract).then_inc(s_bn, 1)
            with V.Fori(0, WINDOWS) as w:
                dve.wait_ge(s_mlp, w + 2)
                V.tensor_tensor(hid[:, bass.ds(w * WB, WB), 0:D], node_ps[:, 0:WB * D].rearrange("p (b f) -> p b f", f=D),
                                feat[:, bass.ds(w * WB, WB), :], ALU.add).then_inc(s_y, 1)
            dve.wait_ge(s_y, WINDOWS + 1)
            link(V.tensor_tensor(X, H, row(LAYERS + 1), ALU.add))
            layer_norm(1)
            V.tensor_tensor(X, X, over(stat[:, 3, :]), ALU.mult).then_inc(s_final, 1)

        @block.scalar
        def _(act):
            A = nc.scalar
            for c in (s_evac[0], s_evac[1], s_place[1], s_dagg, s_dout):
                act.sem_inc(c, 1)
            for c in (gathered_sems.agg, gathered_sems.nodec, *gathered_sems.read, gin_sems.agg, gin_sems.nodec):
                act.sem_inc(c, 1)

            def node_windows(n, e):
                before, wb = steps_before(A, n), windows_before(n)
                with A.Fori(0, WINDOWS) as w:
                    if n == GIN:
                        act.wait_ge(e.node, w + (wb + 1))
                        A.copy(feat_win[:, :, :], feat[:, bass.ds(w * WB, WB), :]).then_inc(e.fwin, 1)
                    first, end = limits(A, w)
                    with A.Fori(first, end) as j:
                        c = j + before
                        for s in range(2):
                            if n < GIN:
                                act.wait_ge(e.rows[n % LAYERS][s], (j + 1) * (16 * UNIT))
                                act.sem_inc(e.read[s], 1)
                            else:
                                act.wait_ge(e.msg[s], c + 2)
                                act.wait_ge(e.sum[s], c + 1)
                                A.activation(rows16[:, s, :, 0:D], msg[:, s, :, :], ACT.Relu).then_inc(e.p1[s], 1)
                                act.wait_ge(e.r1[s], c + 1)
                                A.copy(rows16[:, s, :, D:2 * D], left[:, s, :, :]).then_inc(e.p2[s], 1)
                    act.wait_ge(e.win, w + (wb + 1))
                    act.wait_ge(e.node, w + (wb + 1))
                    A.copy(agg_a[:, :], acc_a[:, :])
                    A.copy(agg_b[:, :], acc_b[:, :]).then_inc(e.agg, 1)
                    act.wait_ge(e.node, w + (wb + 2))
                    if n == GIN:
                        A.activation(hiddenT[:, bass.ds(w * WIN, WIN)], node_ps[0:D, :], ACT.Identity,
                                     bias=cols[:, 0:1]).then_inc(e.nodec, 1)
                    else:
                        A.copy(hid[:, bass.ds(w * WB, WB), :], node_ps[:, 0:WB * (D + 1)].rearrange("p (b f) -> p b f", f=D + 1)).then_inc(e.nodec, 1)

            act.wait_ge(s_bounds, 1)
            act.wait_ge(s_ident, 1)
            A.activation(chosen[:, 0, :], select[:, 0:GPW], ACT.Copy).then_inc(s_place[0], 1)
            with A.Fori(0, WINDOWS) as w:
                for h in range(2):
                    act.wait_ge(s_free[h], w + 1)
                    with A.Fori(0, GPH // 2) as m:
                        q = w * GPH + m + h * (GPH // 2)
                        for s in range(2):
                            act.wait_ge(s_used[s], q * DENSE + 2 * DENSE)
                            act.wait_ge(s_degd[s], q + 1)
                            act.wait_ge(s_place[s], q + 1)
                            A.copy(chosen[:, s, :], select[:, bass.ds(GPW - 1 - s - h * GPH - m * 2, GPW)])
                            A.activation(counted[:, s, :].bitcast(F8).rearrange("p (a c) -> p a c", a=2), group_ps[s], ACT.Copy,
                                         scale=UNIT_COUNT, saturate=False).then_inc(s_evac[s], 1)
                            act.wait_ge(s_evac[s], q + 2)
                            A.copy(win_pairs[h].rearrange("p (b d) -> p b d", b=BLOCKS)[:, :, bass.ds(m * GROUP + s * (GROUP // 2), GROUP // 2)],
                                   counted[:, s, :].bitcast(U16).rearrange("p (b d) -> p b d", b=BLOCKS)).then_inc(s_place[s], 1)
            act.wait_ge(s_degc, 1)
            A.activation(stat[:, 1, 0:BLOCKS], stat[:, 0, 0:BLOCKS], ACT.Sqrt).then_inc(s_sqrt, 1)
            for n in range(LAYERS):
                def dense_window(w, par):
                    act.wait_ge(s_dwin, w + (n * WINDOWS + 1))
                    A.copy(agg_d[par][:, :], acc_d[par]).then_inc(s_dagg, 1)
                    act.wait_ge(s_dnode, w + (n * WINDOWS + 1))
                    A.copy(hid[:, bass.ds(w * WB, WB), 0:D], node_ps[:, 0:WB * (D + 1)].rearrange("p (b f) -> p b f", f=D + 1)[:, :, 0:D]).then_inc(s_dout, 1)

                dense_window(0, 0)
                with A.Fori(0, WINDOWS // 2) as m:
                    dense_window(m * 2 + 1, 1)
                    dense_window(m * 2 + 2, 0)
                if n == 0:
                    act.wait_ge(s_degc, 2)
                    A.activation(stat[:, 1, 0:BLOCKS], stat[:, 0, 0:BLOCKS], ACT.Sqrt).then_inc(s_sqrt, 1)
                act.wait_ge(s_dexp_in, n + 1)
                A.activation(tmp[:, 0:BLOCKS, :], tmp[:, 0:BLOCKS, :], ACT.Exp).then_inc(s_dexp, 1)
            act.wait_ge(s_flag, 1)
            flagged = A.value_load(flag[0:1, 0:1], min_val=0, max_val=1)
            with A.If(flagged > 0):
                act.wait_ge(s_gdeg, 1)
                A.activation(stat[:, 1, 0:BLOCKS], stat[:, 0, 0:BLOCKS], ACT.Sqrt).then_inc(s_gsqrt, 1)
                for n in range(LAYERS):
                    node_windows(n, es[n])
                    if n == 0:
                        act.wait_ge(s_gdeg, 2)
                        A.activation(stat[:, 1, 0:BLOCKS], stat[:, 0, 0:BLOCKS], ACT.Sqrt).then_inc(s_gsqrt, 1)
                    act.wait_ge(s_exp_in, n + 1)
                    A.activation(tmp[:, 0:BLOCKS, :], tmp[:, 0:BLOCKS, :], ACT.Exp).then_inc(s_exp, 1)
            act.wait_ge(s_ln_in, 1)
            A.activation(stat[:, 0, 0:BLOCKS], stat[:, 2, 0:BLOCKS], ACT.Sqrt).then_inc(s_ln, 1)
            act.wait_ge(s_table[GIN], 16)
            node_windows(GIN, es[GIN])
            act.wait_ge(s_bnv, 1)
            A.activation(cols[:, 4:5], cols[:, 3:4], ACT.Sqrt).then_inc(s_bns, 1)
            act.wait_ge(s_bn, 1)
            with A.Fori(0, WINDOWS) as w:
                act.wait_ge(s_mlp, w + 1)
                A.activation(act_win[:, :], hiddenT[:, bass.ds(w * WIN, WIN)], ACT.Relu, bias=cols[:, 7:8],
                             scale=cols[:, 6:7]).then_inc(s_act, 1)
            act.wait_ge(s_ln_in, 2)
            A.activation(stat[:, 0, 0:BLOCKS], stat[:, 2, 0:BLOCKS], ACT.Sqrt).then_inc(s_ln, 1)

        @block.tensor
        def _(pe):
            M = nc.tensor.matmul
            for s in range(2):
                pe.sem_inc(s_used[s], DENSE)
                pe.sem_inc(s_degd[s], 1)
            pe.sem_inc(s_xused, OTHERS)
            for k in range(PIECES):
                pe.sem_inc(s_pused[k], 1)
            for c in (s_hist[0], s_hist[1], es[GIN].ea[0], es[GIN].ea[1], s_mlp):
                pe.sem_inc(c, 1)
            for c in (*gathered_sems.sum, gathered_sems.node, *gin_sems.sum, gin_sems.node):
                pe.sem_inc(c, 1)
            for c in range(FC):
                for n in range(2):
                    pe.wait_ge(s_reach[n], c + 1)
                    for a in range(4):
                        last = M(banks[0:1, 4 * n + a, 0:GROUPS // 4], ones16[0:FOLD, :], reach[0:FOLD, n, a * (GROUPS // 4):(a + 1) * (GROUPS // 4)],
                                 start=(c == 0), stop=(c == FC - 1))
                    last.then_inc(s_count[n], 1)
            pe.wait_ge(s_lims, 1)
            pe.wait_ge(s_tri, 4)
            M(small_ps[0:1, 0:WINDOWS + 1], lims[:, 4:5], tri[:, :], start=True, stop=True)
            M(small_ps[0:1, 32:32 + WINDOWS], lims[:, 4:5], tri[:, 0:WINDOWS], start=True, stop=False)
            M(small_ps[0:1, 32:32 + WINDOWS], lims[:, 5:6], ident[0:WINDOWS, 0:WINDOWS], start=False, stop=True).then_inc(s_bps, 1)
            pe.wait_ge(s_groups, 1)
            pe.wait_ge(s_ident, 1)
            pe.wait_ge(s_bounds, 1)

            def zeros(out, start, rows):
                for a in range(2):
                    last = M(out[:, a, :], zeros16[:, 0:rows], zeros16[:, 0:HALF_BANK], start=start, stop=not start)
                return last

            zeros(out_ps, True, P)
            with nc.tensor.Fori(0, WINDOWS) as w:
                pe.wait_ge(s_inread, w + 1)
                zeros(inwin_ps, True, GPW)

                def counts_of(q, s, more):
                    def tile(slot, start, stop):
                        for a in range(2):
                            last = M(group_ps[s][:, a, :], at(lo_ring, slot), at(key_hot, slot)[:, a * HALF_BANK:(a + 1) * HALF_BANK],
                                     start=start, stop=stop)
                        return last

                    def other(i, t):
                        pe.wait_ge(s_xpair, i + 1)
                        tile(other_slot(i), False, False).then_inc(s_xused, 1)

                    pe.wait_ge(s_evac[s], q + 1)
                    for k in range(DENSE):
                        if k == DENSE - 1:
                            beyond(nc.tensor, q * 2 + s, more[s], other)
                        pe.wait_ge(s_pair[s], q * DENSE + (k + 1))
                        tile(s * DENSE + k, k == 0, k == DENSE - 1).then_inc(s_used[s], 1)

                def degrees_of(q, s):
                    pe.wait_ge(s_evac[s], q + 2)
                    pe.sem_inc(s_turn_pe, 1)
                    group_counts = counted[:, s, :].bitcast(F8).rearrange("p (a c) -> p a c", a=2)
                    for a in range(2):
                        M(out_ps[:, a, :], ident16[:, :], group_counts[:, a, :], start=False, stop=False)
                    for a in range(2):
                        last = M(inwin_ps[:, a, :], chosen[:, s, :], group_counts[:, a, :], start=False, stop=False)
                    last.then_inc(s_degd[s], 1)

                tiles, more, either = pair_word(nc.tensor, w * (GPW // 2))
                counts_of(w * (GPW // 2), 0, more)
                counts_of(w * (GPW // 2), 1, more)
                degrees_of(w * (GPW // 2), 0)
                with nc.tensor.Fori(1, GPW // 2) as m:
                    q = w * (GPW // 2) + m
                    tiles, more, either = pair_word(nc.tensor, q)
                    counts_of(q, 0, more)
                    degrees_of(q - 1, 1)
                    counts_of(q, 1, more)
                    degrees_of(q, 0)
                degrees_of(w * (GPW // 2) + (GPW // 2 - 1), 1)
                zeros(inwin_ps, False, GPW).then_inc(s_inwin, 1)
            zeros(out_ps, False, P).then_inc(s_outdeg, 1)
            pe.wait_ge(s_wd, 1)
            pe.wait_ge(s_bounds, 1)
            for n in range(LAYERS):
                pe.wait_ge(s_max, n + 1)
                M(small_ps[0:1, 0:P], scale[:, 4:5], ident[:, :], start=True, stop=True).then_inc(s_maxt, 1)
                pe.wait_ge(s_pow, n + 1)
                M(small_ps[:, 256:258], ones_f[:, :], pow_row[:, 1:3], start=True, stop=True).then_inc(s_powb, 1)
                pe.wait_ge(s_f16, n + 1)

                def dense_window(w, par):
                    if not (n == 0 and par == 0 and isinstance(w, int)):
                        pe.wait_ge(s_dagg, w + n * WINDOWS)
                    for k in range(PIECES):
                        pe.wait_ge(s_piece[k], w * 16 + (n * WINDOWS + 1) * 16)
                        pe.sem_inc(s_turn_pe, 1)
                        for b in range(PB):
                            hi = k * PB + b
                            moving = pieces[:, k, :, b * HALF:(b + 1) * HALF]
                            last = M(acc_d[par].rearrange("p (h d) -> p h d", h=2), rows_f16[:, hi, :], moving, start=(hi == 0), stop=(hi == BLOCKS - 1))
                        last.then_inc(s_pused[k], 1)
                    pe.drain().then_inc(s_dwin, 1)

                def nodes(w, par):
                    pe.wait_ge(s_dagg, w + (n * WINDOWS + 2))
                    pe.wait_ge(s_dout, w + (n * WINDOWS + 1))
                    for c in range(WB):
                        last = M(node_ps[:, c * (D + 1):c * (D + 1) + D], agg_d[par][:, c * P:(c + 1) * P], w_d[:, n, :], start=True, stop=True)
                    last.then_inc(s_dnode, 1)

                dense_window(0, 0)
                with nc.tensor.Fori(0, WINDOWS // 2) as m:
                    dense_window(m * 2 + 1, 1)
                    nodes(m * 2, 0)
                    dense_window(m * 2 + 2, 0)
                    nodes(m * 2 + 1, 1)
                nodes(WINDOWS - 1, 0)
                if n == 0:
                    pe.wait_ge(s_inback, 16)
                    M(small_ps[:, 384:384 + PADDED], in_rows, ident[0:PADDED, 0:PADDED], start=True, stop=True)
                    pe.wait_ge(s_flagin, 1)
                    M(small_ps[0:1, 300:301], scale[:, 5:6], ones_col[:, :], start=True, stop=True).then_inc(s_flagsum, 1)

            def edge_term(s):
                M(edge_ps[s][:, 0:UNIT * D], attr_sb[:, s, :], w_edge_blk[:, :, :].rearrange("p k f -> p (k f)"),
                  start=True, stop=True).then_inc(es[GIN].ea[s], 1)

            def edge_sums(n):
                e = es[n]
                before, wb = steps_before(nc.tensor, n), windows_before(n)
                if n == GIN:
                    for s in range(2):
                        pe.wait_ge(e.attr[s], 16)
                        edge_term(s)
                with nc.tensor.Fori(0, WINDOWS) as w:
                    first, end = limits(nc.tensor, w)
                    pe.wait_ge(e.agg, w + (wb + 1))
                    M(acc_a[:, :], zeros16[:, 0:P], zeros16[:, :], start=True, stop=False)
                    M(acc_b[:, :], zeros16[:, 0:P], zeros16[:, :], start=True, stop=False)
                    if n == GIN:
                        pe.wait_ge(e.fwin, w + (wb + 1))
                        for b in range(WB):
                            M(acc_b[0:D, b * P:(b + 1) * P], feat_win[:, b, :], ident[:, :], start=False, stop=False)
                    with nc.tensor.Fori(first, end) as j:
                        c = j + before
                        for s in range(2):
                            pe.wait_ge(e.hot[s], c + 1)
                            if n == GIN:
                                pe.wait_ge(e.p3[s], c + 2)
                            else:
                                pe.wait_ge(e.rows[n % LAYERS][s], (j + 1) * (16 * UNIT))
                            for k in range(UNIT):
                                M(acc_a[:, :], rows16[:, s, k, 0:P], onehot[:, s, k, :], start=False, stop=False)
                                last = M(acc_b[:, :], rows16[:, s, k, P:2 * P], onehot[:, s, k, :], start=False, stop=False)
                            last.then_inc(e.sum[s], 1)
                            if n == GIN:
                                pe.wait_ge(e.attr[s], (c + 2) * 16)
                                pe.wait_ge(e.msg[s], c + 2)
                                edge_term(s)
                    M(acc_a[:, :], zeros16[:, 0:P], zeros16[:, :], start=False, stop=True)
                    M(acc_b[:, :], zeros16[:, 0:P], zeros16[:, :], start=False, stop=True).then_inc(e.win, 1)
                    pe.wait_ge(e.agg, w + (wb + 2))
                    pe.wait_ge(e.nodec, w + (wb + 1))
                    if n == GIN:
                        M(node_ps[0:D, :], w1_a[:, :], agg_a[:, :], start=True, stop=False)
                        M(node_ps[0:D, :], w1_a[0:D, :], agg_b[0:D, :], start=False, stop=True).then_inc(e.node, 1)
                    else:
                        for b in range(WB):
                            o = node_ps[:, b * (D + 1):(b + 1) * (D + 1)]
                            M(o, agg_a[:, b * P:(b + 1) * P], w_a[:, n, :], start=True, stop=False)
                            last = M(o, agg_b[:, b * P:(b + 1) * P], w_b[:, n, :], start=False, stop=True)
                        last.then_inc(e.node, 1)

            pe.wait_ge(s_flag, 1)
            flagged = nc.tensor.value_load(flag[0:1, 0:1], min_val=0, max_val=1)
            with nc.tensor.If(flagged > 0):
                M(deg_ps[:, 0:BLOCKS], zeros16[:, 0:P], zeros16[:, 0:BLOCKS], start=True, stop=False)
                with nc.tensor.Fori(0, GRANULES) as g:
                    for s in range(2):
                        pe.wait_ge(s_hot[s], g + 1)
                        for k in range(UNIT):
                            last = M(deg_ps[:, 0:BLOCKS], lo_hot[:, s, k, :], hi_hot[:, s, k, :], start=False, stop=False)
                        last.then_inc(s_hist[s], 1)
                M(deg_ps[:, 0:BLOCKS], zeros16[:, 0:P], zeros16[:, 0:BLOCKS], start=False, stop=True).then_inc(s_deg, 1)
                for n in range(LAYERS):
                    edge_sums(n)
            edge_sums(GIN)
            pe.wait_ge(es[GIN].nodec, WINDOWS + 1)
            with nc.tensor.Fori(0, WINDOWS) as w:
                pe.wait_ge(s_act, w + 1)
                pe.wait_ge(s_y, w + 1)
                for c in range(WB):
                    last = M(node_ps[:, c * D:(c + 1) * D], act_win[:, c * P:(c + 1) * P], w2_sb[:, :], start=True, stop=True)
                last.then_inc(s_mlp, 1)


def kernel(x, src, dst, edge_attr_16, L0_gnn_W0, L0_gnn_b0, L0_gnn_W1, L0_gnn_b1, L0_gnn_W2, L0_gnn_b2,
           L1_gnn_W_edge, L1_gnn_b_edge, L1_gnn_W1, L1_gnn_b1, L1_gnn_gamma, L1_gnn_beta, L1_gnn_W2, L1_gnn_b2):
    import numpy as np
    import concourse.bacc as bacc
    from concourse.bass_utils import run_bass_kernel_spmd

    laid_out = {
        "x": np.asarray(x),
        "src": np.asarray(src).reshape(TILES, P).T,
        "dst": np.asarray(dst).reshape(TILES, P).T,
        "dst_tiles": np.asarray(dst).reshape(FOLD, TILES // FOLD * P),
        "dst_back": np.asarray(dst)[::-1].reshape(FOLD, TILES // FOLD * P),
        "attr": np.asarray(edge_attr_16).reshape(UNITS, UNIT, P, EDIM).transpose(0, 1, 3, 2).reshape(UNITS, UNIT * EDIM, P),
        "w_l0": np.stack([np.asarray(w) for w in (L0_gnn_W0, L0_gnn_W1, L0_gnn_W2)]),
        "b_l0": np.stack([np.asarray(b) for b in (L0_gnn_b0, L0_gnn_b1, L0_gnn_b2)]).reshape(LAYERS, 1, D),
        "w_edge": np.asarray(L1_gnn_W_edge).T,
        "b_edge": np.asarray(L1_gnn_b_edge).reshape(1, D),
        "w1": np.asarray(L1_gnn_W1).T,
        "b1": np.asarray(L1_gnn_b1).reshape(D, 1),
        "gamma": np.asarray(L1_gnn_gamma).reshape(D, 1),
        "beta": np.asarray(L1_gnn_beta).reshape(D, 1),
        "w2": np.asarray(L1_gnn_W2).T,
        "b2": np.asarray(L1_gnn_b2).reshape(1, D),
    }
    nc = bacc.Bacc("TRN2", target_bir_lowering=False, num_devices=1)
    arrays = {f"{name}_dram": np.ascontiguousarray(a) for name, a in laid_out.items()}
    args = [nc.dram_tensor(name, a.shape, mybir.dt.from_np(a.dtype), kind="ExternalInput").ap() for name, a in arrays.items()]
    out = nc.dram_tensor("out_dram", (NODES, D), F32, kind="ExternalOutput").ap()
    gnn_kernel(nc, *args, out)
    return run_bass_kernel_spmd(nc, [arrays], core_ids=[0]).results[0]["out_dram"]
```
